# Optimizing a Trainium2 kernel written in Bass

```python
import numpy as np
import jax
import jax.numpy as jnp

def _softmax(x, axis=-1):
    return jax.nn.softmax(x, axis=axis)

def _gelu(x):
    return jax.nn.gelu(x, approximate=True)

def _silu(x):
    return jax.nn.silu(x)

def _sigmoid(x):
    return jax.nn.sigmoid(x)

def _layernorm(x, axis=-1, eps=1e-05):
    m = jnp.mean(x, axis=axis, keepdims=True)
    v = jnp.var(x, axis=axis, keepdims=True)
    return (x - m) / jnp.sqrt(v + eps)

def _scatter_add(tgt, idx, src, axis=0):
    return tgt.at[idx].add(src)

def _segment_sum(src, seg, n):
    return jax.ops.segment_sum(src, seg, n)
kernel_name = 'mk_prb_d1_jaxref_r8_3b4b7d'

def setup_inputs(seed: int=0):
    np.random.seed(seed)
    _w = jnp.asarray

    def _L0_attn_setup():
        import math
        import jax, jax.numpy as jnp
        import numpy as np
        D_MODEL = 128
        N_HEADS = 16
        D_HEAD = D_MODEL // N_HEADS

        def get_alibi_slopes(n_heads: int) -> np.ndarray:

            def pow2_slopes(n):
                start = 2 ** (-2 ** (-(math.log2(n) - 3)))
                return np.array([start * start ** i for i in range(n)], dtype=np.float32)
            if math.log2(n_heads).is_integer():
                return pow2_slopes(n_heads)
            closest = 2 ** math.floor(math.log2(n_heads))
            slopes = pow2_slopes(closest)
            extra = pow2_slopes(2 * closest)[0::2][:n_heads - closest]
            return np.concatenate([slopes, extra], axis=0)
        key = jax.random.key(seed)
        ks = jax.random.split(key, 9)
        B, S, D = (2, 256, D_MODEL)
        scale = 1.0 / math.sqrt(D)
        inp = {'x': jax.random.normal(ks[0], (B, S, D), dtype=jnp.float32), 'Wq': jax.random.normal(ks[1], (D, D), dtype=jnp.float32) * scale, 'bq': jnp.zeros((D,), dtype=jnp.float32), 'Wk': jax.random.normal(ks[2], (D, D), dtype=jnp.float32) * scale, 'bk': jnp.zeros((D,), dtype=jnp.float32), 'Wv': jax.random.normal(ks[3], (D, D), dtype=jnp.float32) * scale, 'bv': jnp.zeros((D,), dtype=jnp.float32), 'Wo': jax.random.normal(ks[4], (D, D), dtype=jnp.float32) * scale, 'bo': jnp.zeros((D,), dtype=jnp.float32)}
        return inp
    _L0_attn_in = _L0_attn_setup()

    def _L0_ffn_setup():
        import jax, jax.numpy as jnp
        import numpy as np
        N_EXPERTS = 32
        TOP_K = 8
        N_GROUP = 4
        TOPK_GROUP = 2
        ROUTED_SCALING = 2.5

        def _gate(x, gate_w, gate_bias):
            T, E = (x.shape[0], gate_w.shape[0])
            logits = jnp.einsum('th,eh->te', x, gate_w)
            scores = jax.nn.sigmoid(logits)
            scores_choice = scores + gate_bias[None, :]
            grp = scores_choice.reshape(T, N_GROUP, E // N_GROUP)
            top2, _ = jax.lax.top_k(grp, 2)
            group_scores = top2.sum(-1)
            _, grp_idx = jax.lax.top_k(group_scores, TOPK_GROUP)
            group_mask = jax.nn.one_hot(grp_idx, N_GROUP, dtype=scores.dtype).sum(1)
            expert_mask = jnp.repeat(group_mask, E // N_GROUP, axis=1)
            masked = jnp.where(expert_mask > 0, scores_choice, 0.0)
            _, topk_idx = jax.lax.top_k(masked, TOP_K)
            topk_w = jnp.take_along_axis(scores, topk_idx, axis=1)
            topk_w = topk_w / (topk_w.sum(-1, keepdims=True) + 1e-20)
            topk_w = topk_w * ROUTED_SCALING
            return (topk_idx, topk_w)

        def _mlp(x, wg, wu, wd):
            return jnp.einsum('...i,hi->...h', jax.nn.silu(jnp.einsum('...h,ih->...i', x, wg)) * jnp.einsum('...h,ih->...i', x, wu), wd)
        key = jax.random.key(seed)
        ks = jax.random.split(key, 9)
        B, S, H, I = (2, 64, 128, 64)
        w = 0.02
        return {'hidden_states': jax.random.normal(ks[0], (B, S, H), jnp.float32), 'gate_w': jax.random.normal(ks[1], (N_EXPERTS, H), jnp.float32) * w, 'gate_bias': jax.random.normal(ks[2], (N_EXPERTS,), jnp.float32) * w, 'expert_gate': jax.random.normal(ks[3], (N_EXPERTS, I, H), jnp.float32) * w, 'expert_up': jax.random.normal(ks[4], (N_EXPERTS, I, H), jnp.float32) * w, 'expert_down': jax.random.normal(ks[5], (N_EXPERTS, H, I), jnp.float32) * w, 'shared_gate': jax.random.normal(ks[6], (2 * I, H), jnp.float32) * w, 'shared_up': jax.random.normal(ks[7], (2 * I, H), jnp.float32) * w, 'shared_down': jax.random.normal(ks[8], (H, 2 * I), jnp.float32) * w}
    _L0_ffn_in = _L0_ffn_setup()
    _d = {'L0_attn_x': _L0_attn_in['x'], 'L0_attn_Wq': _L0_attn_in['Wq'], 'L0_attn_bq': _L0_attn_in['bq'], 'L0_attn_Wk': _L0_attn_in['Wk'], 'L0_attn_bk': _L0_attn_in['bk'], 'L0_attn_Wv': _L0_attn_in['Wv'], 'L0_attn_bv': _L0_attn_in['bv'], 'L0_attn_Wo': _L0_attn_in['Wo'], 'L0_attn_bo': _L0_attn_in['bo'], 'L0_ffn_gate_w': _L0_ffn_in['gate_w'], 'L0_ffn_gate_bias': _L0_ffn_in['gate_bias'], 'L0_ffn_expert_gate': _L0_ffn_in['expert_gate'], 'L0_ffn_expert_up': _L0_ffn_in['expert_up'], 'L0_ffn_expert_down': _L0_ffn_in['expert_down'], 'L0_ffn_shared_gate': _L0_ffn_in['shared_gate'], 'L0_ffn_shared_up': _L0_ffn_in['shared_up'], 'L0_ffn_shared_down': _L0_ffn_in['shared_down']}
    _x0 = _d['L0_attn_x']
    _d['L0_attn_x'] = jax.random.normal(jax.random.fold_in(jax.random.key(seed), 1), (16, 512, 128), dtype=_x0.dtype)
    del _x0
    return _d

def reference(L0_attn_x, L0_attn_Wq, L0_attn_bq, L0_attn_Wk, L0_attn_bk, L0_attn_Wv, L0_attn_bv, L0_attn_Wo, L0_attn_bo, L0_ffn_gate_w, L0_ffn_gate_bias, L0_ffn_expert_gate, L0_ffn_expert_up, L0_ffn_expert_down, L0_ffn_shared_gate, L0_ffn_shared_up, L0_ffn_shared_down):

    def _L0_attn_ref(x, Wq, bq, Wk, bk, Wv, bv, Wo, bo):
        import math
        import jax, jax.numpy as jnp
        import numpy as np
        D_MODEL = 128
        N_HEADS = 16
        D_HEAD = D_MODEL // N_HEADS

        def get_alibi_slopes(n_heads: int) -> np.ndarray:

            def pow2_slopes(n):
                start = 2 ** (-2 ** (-(math.log2(n) - 3)))
                return np.array([start * start ** i for i in range(n)], dtype=np.float32)
            if math.log2(n_heads).is_integer():
                return pow2_slopes(n_heads)
            closest = 2 ** math.floor(math.log2(n_heads))
            slopes = pow2_slopes(closest)
            extra = pow2_slopes(2 * closest)[0::2][:n_heads - closest]
            return np.concatenate([slopes, extra], axis=0)
        B, S, D = x.shape
        H, Dh = (N_HEADS, D_HEAD)
        q = (x @ Wq.T + bq).reshape(B, S, H, Dh).transpose(0, 2, 1, 3)
        k = (x @ Wk.T + bk).reshape(B, S, H, Dh).transpose(0, 2, 1, 3)
        v = (x @ Wv.T + bv).reshape(B, S, H, Dh).transpose(0, 2, 1, 3)
        scores = jnp.einsum('bhqd,bhkd->bhqk', q, k) / math.sqrt(Dh)
        slopes = jnp.asarray(get_alibi_slopes(H), dtype=scores.dtype)
        pos = jnp.arange(S, dtype=scores.dtype)
        pos_diff = pos[None, :] - pos[:, None]
        alibi = slopes[:, None, None] * pos_diff[None, :, :]
        scores = scores + alibi[None]
        causal = jnp.tril(jnp.ones((S, S), dtype=bool))
        scores = jnp.where(causal[None, None], scores, -jnp.inf)
        weights = jax.nn.softmax(scores, axis=-1)
        y = jnp.einsum('bhqk,bhkd->bhqd', weights, v)
        y = y.transpose(0, 2, 1, 3).reshape(B, S, D)
        return y @ Wo.T + bo

    def _L0_ffn_ref(hidden_states, gate_w, gate_bias, expert_gate, expert_up, expert_down, shared_gate, shared_up, shared_down):
        import jax, jax.numpy as jnp
        import numpy as np
        N_EXPERTS = 32
        TOP_K = 8
        N_GROUP = 4
        TOPK_GROUP = 2
        ROUTED_SCALING = 2.5

        def _gate(x, gate_w, gate_bias):
            T, E = (x.shape[0], gate_w.shape[0])
            logits = jnp.einsum('th,eh->te', x, gate_w)
            scores = jax.nn.sigmoid(logits)
            scores_choice = scores + gate_bias[None, :]
            grp = scores_choice.reshape(T, N_GROUP, E // N_GROUP)
            top2, _ = jax.lax.top_k(grp, 2)
            group_scores = top2.sum(-1)
            _, grp_idx = jax.lax.top_k(group_scores, TOPK_GROUP)
            group_mask = jax.nn.one_hot(grp_idx, N_GROUP, dtype=scores.dtype).sum(1)
            expert_mask = jnp.repeat(group_mask, E // N_GROUP, axis=1)
            masked = jnp.where(expert_mask > 0, scores_choice, 0.0)
            _, topk_idx = jax.lax.top_k(masked, TOP_K)
            topk_w = jnp.take_along_axis(scores, topk_idx, axis=1)
            topk_w = topk_w / (topk_w.sum(-1, keepdims=True) + 1e-20)
            topk_w = topk_w * ROUTED_SCALING
            return (topk_idx, topk_w)

        def _mlp(x, wg, wu, wd):
            return jnp.einsum('...i,hi->...h', jax.nn.silu(jnp.einsum('...h,ih->...i', x, wg)) * jnp.einsum('...h,ih->...i', x, wu), wd)
        orig_shape = hidden_states.shape
        H = orig_shape[-1]
        residuals = hidden_states
        x = hidden_states.reshape(-1, H)
        topk_idx, topk_w = _gate(x, gate_w, gate_bias)
        g = jnp.einsum('th,eih->eti', x, expert_gate)
        u = jnp.einsum('th,eih->eti', x, expert_up)
        outs = jnp.einsum('eti,ehi->eth', jax.nn.silu(g) * u, expert_down)
        outs_t = jnp.transpose(outs, (1, 0, 2))
        gathered = jnp.take_along_axis(outs_t, topk_idx[:, :, None], axis=1)
        final = (gathered * topk_w[:, :, None]).sum(1)
        shared = _mlp(residuals, shared_gate, shared_up, shared_down)
        return final.reshape(orig_shape) + shared
    x = L0_attn_x
    xn = _layernorm(x, axis=-1)
    x = x + _L0_attn_ref(xn, L0_attn_Wq, L0_attn_bq, L0_attn_Wk, L0_attn_bk, L0_attn_Wv, L0_attn_bv, L0_attn_Wo, L0_attn_bo) + _L0_ffn_ref(xn, L0_ffn_gate_w, L0_ffn_gate_bias, L0_ffn_expert_gate, L0_ffn_expert_up, L0_ffn_expert_down, L0_ffn_shared_gate, L0_ffn_shared_up, L0_ffn_shared_down)
    return x

_drawn_inputs = setup_inputs


def setup_inputs(seed=0):
    import zlib

    import numpy as np

    out = dict(_drawn_inputs(seed))
    spreads = {'L0_attn_bq': (0.0, 1.715),
     'L0_attn_bk': (0.0, 2.0),
     'L0_attn_bv': (0.0, 0.399),
     'L0_attn_bo': (0.0, 0.376)}
    factors = {'L0_ffn_gate_w': 8.0,
     'L0_ffn_gate_bias': 8.0,
     'L0_ffn_expert_gate': 8.0,
     'L0_ffn_expert_up': 8.0,
     'L0_ffn_expert_down': 8.0,
     'L0_ffn_shared_gate': 8.0,
     'L0_ffn_shared_up': 8.0,
     'L0_ffn_shared_down': 8.0}
    for name, (base, spread) in spreads.items():
        noise = np.random.default_rng([zlib.crc32(name.encode()), seed]).standard_normal(out[name].shape)
        drawn = base * np.exp(spread * noise) if base else spread * noise
        out[name] = jnp.asarray(drawn.astype(out[name].dtype))
    for name, factor in factors.items():
        out[name] = (out[name] * factor).astype(out[name].dtype)
    return out
```

```python
from contextlib import ExitStack

import numpy as np

import concourse.bass as bass
from concourse import mybir

F32 = mybir.dt.float32
F32R = mybir.dt.float32r
ALU = mybir.AluOpType
ACT = mybir.ActivationFunctionType
AX = mybir.AxisListType

P = 128
B, S, D = 16, 512, 128
TILES = S // P
HEADS, DH = 16, 8
PER, GROUPS = 4, 4
E, I = 32, 64
N_GROUP, TOP_K = 4, 8
PER_GROUP = E // N_GROUP
ROUTED_SCALING = 2.5
EPS = 1e-5
PAIRS = E // 2
UNITS = PAIRS + 1
NEVER = -3e38
PREP_INPUTS, PREP_LOGITS, PREP_WEIGHTS = 5, 8, 15

C_IDENT = 0
C_NEG_W = C_IDENT + P
C_NEG_Q = C_NEG_W + 1
C_NEG_K = C_NEG_Q + 1
C_NEG_AUX = C_NEG_K + 1
C_RANK = C_NEG_AUX + 1
C_POW = C_RANK + TILES * N_GROUP
C_MASK_Q = C_POW + TILES
C_MASK_K = C_MASK_Q + P
C_AUX = C_MASK_K + P
C_END = C_AUX + S


def expert_phase(nc, t, dram):
    with ExitStack() as ctx:
        def sb(name, shape, dt=F32):
            return ctx.enter_context(nc.sbuf_tensor(name, shape, dt))

        def psum(name, shape):
            return ctx.enter_context(nc.psum_tensor(name, shape, F32))

        def sem(name):
            return ctx.enter_context(nc.semaphore(name))

        x_rows, xt_hi, xt_lo, const = t["x_rows"], t["xt_hi"], t["xt_lo"], t["const"]
        ident = const[:, C_IDENT:C_IDENT + P]
        WIDE = PAIRS * P
        wg_raw, wu_raw = sb("wg_raw", [P, WIDE + P]), sb("wu_raw", [P, WIDE + P])
        wg_hi, wg_lo = sb("wg_hi", [P, WIDE + P], F32R), sb("wg_lo", [P, WIDE + P], F32R)
        wu_hi, wu_lo = sb("wu_hi", [P, WIDE + P], F32R), sb("wu_lo", [P, WIDE + P], F32R)
        wd = sb("wd", [P, UNITS, D])
        gate_w = sb("gate_w", [P, E])
        gate_b = sb("gate_b", [P, TILES, E])
        bo = sb("bo", [P, 1])
        pick_raw = wg_raw[0:2 * E, 0:PAIRS * P]
        pick = sb("pick", [2 * E, PAIRS, P], F32R)

        stats = sb("stats", [P, TILES, 6])
        mean_var = sb("mean_var", [P, TILES, 2])
        var_eps = sb("var_eps", [P, TILES])
        rstd = sb("rstd", [P, TILES])
        xn = sb("xn", [P, TILES, D])
        xt_raw = sb("xt_raw", [P, S])
        th = sb("th", [P, TILES, E])
        scores = sb("scores", [P, TILES, E])
        choice = sb("choice", [P, TILES, E])
        TG = TILES * N_GROUP
        hi1, lo1 = sb("hi1", [P, TG, 4]), sb("lo1", [P, TG, 4])
        hi2, lo2a = sb("hi2", [P, TG, 2]), sb("lo2a", [P, TG, 2])
        lo2b, lo2 = sb("lo2b", [P, TG, 2]), sb("lo2", [P, TG, 2])
        hi3, lo3a = sb("hi3", [P, TG]), sb("lo3a", [P, TG])
        lo3b, lo3 = sb("lo3b", [P, TG]), sb("lo3", [P, TG])
        group_score = sb("group_score", [P, TILES, N_GROUP])
        beats = [sb(f"beats{d}", [P, TILES, N_GROUP + d]) for d in (1, 2, 3)]
        net = [sb(f"net{d}", [P, TILES, N_GROUP]) for d in (1, 2, 3)]
        group_on = sb("group_on", [P, TILES, N_GROUP])
        masked = sb("masked", [P, TILES, E])
        top8 = sb("top8", [P, TILES, TOP_K])
        taken = sb("taken", [P, TILES, E])
        chosen = sb("chosen", [P, TILES, E])
        w_sum = sb("w_sum", [P, TILES])
        spare = sb("spare", [P, 1])
        w_row = sb("w_row", [P, TILES, 2, E])
        wt_round = sb("wt_round", [2 * E, S], F32R)
        wt = sb("wt", [2 * E, S], F32R)

        silu = [sb(f"silu{n}", [P, S]) for n in range(2)]
        hidden = sb("hidden", [P, S])
        weighted = [sb(f"weighted{n}", [P, S]) for n in range(2)]
        ffn_t = sb("ffn_t", [D, S])

        gate_ps = [psum(f"gate_ps{n}", [P, S]) for n in range(2)]
        up_ps = [psum(f"up_ps{n}", [P, S]) for n in range(2)]
        spread_ps = [psum(f"spread_ps{n}", [P, S]) for n in range(2)]
        ffn_ps = psum("ffn_ps", [P, S])
        prep_ps = psum("prep_ps", [P, S])

        x_in = [sem("x_in0"), sem("x_in1")]
        const_in = sem("const_in")
        small_in = sem("small_in")
        pick_in = sem("pick_in")
        wg_in, wu_in, wd_in = sem("wg_in"), sem("wu_in"), sem("wd_in")
        zeroed = sem("zeroed")
        w_rounded = sem("w_rounded")
        w_split = sem("w_split")
        picked = sem("picked")
        has_var, has_rstd, has_xn = sem("has_var"), sem("has_rstd"), sem("has_xn")
        has_xt = sem("has_xt")
        has_w_row = sem("has_w_row")
        has_wt_round = sem("has_wt_round")
        step = sem("step")
        prep_full, prep_free = sem("prep_full"), sem("prep_free")
        gate_full, gate_free = sem("gate_full"), sem("gate_free")
        up_full, up_free = sem("up_full"), sem("up_free")
        spread_full, spread_free = sem("spread_full"), sem("spread_free")
        ffn_free = sem("ffn_free")
        weighted_full, weighted_free = sem("weighted_full"), sem("weighted_free")

        PREP_USES = 4
        W_EARLY = 4

        block = ctx.enter_context(nc.Block())

        @block.sync
        def _(sp):
            sp.dma_start(const[:, :], dram["const"]).then_inc(const_in, 16)
            for b in range(2):
                at = slice(b * TILES, (b + 1) * TILES)
                sp.dma_start(x_rows[:, at, :], dram["x"][:, at, :]).then_inc(x_in[b], 16)
            sp.dma_start(gate_w[:, :], dram["gate_w"]).then_inc(small_in, 16)
            sp.dma_start(gate_b[:, :, :], dram["gate_b"]).then_inc(small_in, 16)
            sp.dma_start(bo[:, :], dram["bo"]).then_inc(small_in, 16)
            sp.dma_start(wg_raw[:, :], dram["wg"]).then_inc(wg_in, 16)
            sp.dma_start(wu_raw[:, :], dram["wu"]).then_inc(wu_in, 16)
            sp.dma_start(wd[:, :, :], dram["wd"]).then_inc(wd_in, 16)
            sp.wait_ge(w_split, 1)
            sp.dma_start(pick_raw, dram["pick"]).then_inc(pick_in, 16)
            with sp.Fori(1, B // 2) as it:
                for half in range(2):
                    sp.wait_ge(x_in[half], it * 16)
                    at = bass.ds((it * 2 + half) * TILES, TILES)
                    sp.dma_start(x_rows[:, at, :], dram["x"][:, at, :]).then_inc(x_in[half], 16)
            sp.wait_ge(x_in[0], B // 2 * 16)
            sp.dma_start(x_rows[:, B * TILES:, :], dram["x"][:, 0:TILES, :]).then_inc(x_in[0], 16)

        @block.gpsimd
        def _(pool):
            for d in range(3):
                pool.memset(beats[d][:, :, :], 0.0).then_inc(zeroed, 1)
            pool.wait_ge(const_in, 16)

            def inverse_deviation(count):
                pool.wait_ge(has_var, count)
                pool.tensor_tensor(rstd[:, :], var_eps[:, :], const[:, C_POW:C_POW + TILES], ALU.pow).then_inc(has_rstd, 1)

            inverse_deviation(1)
            with pool.Fori(0, B) as b:
                inverse_deviation(b + 2)

        @block.scalar
        def _(act):
            act.sem_inc(gate_free, 2)
            act.sem_inc(ffn_free, 1)

            def copy_inputs(n, splits):
                if splits is not None:
                    act.wait_ge(has_xt, splits)
                act.wait_ge(prep_full, n)
                act.copy(xt_raw[:, :], prep_ps[:, :]).then_inc(prep_free, 1)

            def gate_tanh(n):
                act.wait_ge(prep_full, n)
                act.activation(th[:, :, :].rearrange("p t e -> p (t e)"), prep_ps[:, 0:TILES * E], ACT.Tanh, scale=0.5).then_inc(prep_free, 1)

            def round_weights(n):
                act.wait_ge(prep_full, n)
                act.copy(wt_round[:, :], prep_ps[0:2 * E, :]).then_inc(has_wt_round, 1)

            copy_inputs(1, None)
            gate_tanh(2)
            act.wait_ge(wg_in, 16)
            act.copy(wg_hi[:, :], wg_raw[:, :]).then_inc(w_rounded, 1)
            act.wait_ge(wu_in, 16)
            act.copy(wu_hi[:, :], wu_raw[:, :]).then_inc(w_rounded, 1)
            act.wait_ge(small_in, 48)
            act.wait_ge(pick_in, 16)
            act.copy(pick[:, :, :].rearrange("p a b -> p (a b)"), pick_raw).then_inc(picked, 1)
            round_weights(3)

            def finish_ffn(b):
                act.wait_ge(weighted_free, (b + 1) * UNITS + 2)
                act.wait_ge(prep_free, b * PREP_USES + W_EARLY + 1)
                act.activation(ffn_t[:, :], ffn_ps[:, :], ACT.Identity, bias=bo[:, 0:1]).then_inc(ffn_free, 1)

            with act.Fori(0, B // 2) as it:
                for half in range(2):
                    b = it * 2 + half
                    uses = b * PREP_USES + W_EARLY
                    for u in range(UNITS):
                        k = half * UNITS + u
                        done = it * (2 * UNITS) + k
                        act.wait_ge(gate_full, done + 1)
                        act.wait_ge(up_free, done + 1)
                        act.activation(silu[k % 2][:, :], gate_ps[k % 2][:, :], ACT.Silu).then_inc(gate_free, 1)
                        if k == UNITS:
                            finish_ffn(it * 2)
                        if u == PREP_INPUTS:
                            copy_inputs(uses + 1, b + 1)
                        if u == PREP_LOGITS:
                            gate_tanh(uses + 2)
                        if u == PREP_WEIGHTS:
                            round_weights(uses + 3)
                finish_ffn(it * 2 + 1)

        @block.vector
        def _(dve):
            V = nc.vector
            dve.sem_inc(prep_free, 1)
            dve.sem_inc(up_free, 2)
            dve.sem_inc(spread_free, 2)
            count = [0, 0]

            def then(instruction):
                instruction.then_inc(step, 1)
                count[1] += 1
                dve.wait_ge(step, count[0] + count[1])

            def variance(b):
                rows = x_rows[:, bass.ds(b * TILES, TILES), :]
                for i in range(TILES):
                    last = V.bn_stats(stats[:, i, :], rows[:, i, :])
                then(last)
                V.memset(spare[:, :], 0.0)
                for i in range(TILES):
                    last = V.bn_aggr(mean_var[:, i, :], stats[:, i, :])
                then(last)
                V.tensor_scalar(var_eps[:, :], mean_var[:, :, 1], EPS, None, ALU.add).then_inc(has_var, 1)

            def normalise(b, n):
                rows = x_rows[:, bass.ds(b * TILES, TILES), :]
                dve.wait_ge(has_rstd, n)
                for i in range(TILES):
                    last = V.tensor_scalar(xn[:, i, :], rows[:, i, :], mean_var[:, i, 0:1], rstd[:, i:i + 1], ALU.subtract, ALU.mult)
                last.then_inc(has_xn, 1)

            def split_inputs(b, n):
                dve.wait_ge(prep_free, n)
                at = bass.ds(b * S, S)
                then(V.tensor_copy(xt_hi[:, at], xt_raw[:, :]))
                V.tensor_tensor(xt_lo[:, at], xt_raw[:, :], xt_hi[:, at].bitcast(F32), ALU.subtract).then_inc(has_xt, 1)

            def grp(a):
                return a[:, :, :].rearrange("p t (g e) -> p (t g) e", g=N_GROUP)

            def group_scores(n):
                dve.wait_ge(prep_free, n)
                then(V.tensor_scalar(scores[:, :, :], th[:, :, :], 0.5, 0.5, ALU.mult, ALU.add))
                then(V.tensor_tensor(choice[:, :, :], scores[:, :, :], gate_b[:, :, :], ALU.add))
                c = grp(choice)
                V.tensor_tensor(hi1[:, :, :], c[:, :, 0:4], c[:, :, 4:8], ALU.max)
                then(V.tensor_tensor(lo1[:, :, :], c[:, :, 0:4], c[:, :, 4:8], ALU.min))
                V.tensor_tensor(hi2[:, :, :], hi1[:, :, 0:2], hi1[:, :, 2:4], ALU.max)
                V.tensor_tensor(lo2a[:, :, :], hi1[:, :, 0:2], hi1[:, :, 2:4], ALU.min)
                then(V.tensor_tensor(lo2b[:, :, :], lo1[:, :, 0:2], lo1[:, :, 2:4], ALU.max))
                then(V.tensor_tensor(lo2[:, :, :], lo2a[:, :, :], lo2b[:, :, :], ALU.max))
                V.tensor_tensor(hi3[:, :], hi2[:, :, 0], hi2[:, :, 1], ALU.max)
                V.tensor_tensor(lo3a[:, :], hi2[:, :, 0], hi2[:, :, 1], ALU.min)
                then(V.tensor_tensor(lo3b[:, :], lo2[:, :, 0], lo2[:, :, 1], ALU.max))
                then(V.tensor_tensor(lo3[:, :], lo3a[:, :], lo3b[:, :], ALU.max))
                then(V.tensor_tensor(group_score[:, :, :].rearrange("p t g -> p (t g)"), hi3[:, :], lo3[:, :], ALU.add))

            def choose_groups():
                g = group_score
                for d in (1, 2, 3):
                    last = V.tensor_tensor(beats[d - 1][:, :, d:N_GROUP], g[:, :, 0:N_GROUP - d], g[:, :, d:N_GROUP], ALU.is_ge)
                then(last)
                for d in (1, 2, 3):
                    last = V.tensor_tensor(net[d - 1][:, :, :], beats[d - 1][:, :, d:N_GROUP + d], beats[d - 1][:, :, 0:N_GROUP], ALU.subtract)
                then(last)
                then(V.tensor_tensor(net[0][:, :, :], net[0][:, :, :], net[1][:, :, :], ALU.add))
                then(V.tensor_tensor(net[0][:, :, :], net[0][:, :, :], net[2][:, :, :], ALU.add))
                rank = const[:, C_RANK:C_RANK + TG].rearrange("p (t g) -> p t g", t=TILES)
                then(V.tensor_tensor(group_on[:, :, :], net[0][:, :, :], rank, ALU.is_ge))
                on = group_on[:, :, :].rearrange("p t g -> p (t g)").unsqueeze(2).to_broadcast([P, TG, PER_GROUP])
                then(V.tensor_tensor(grp(masked), grp(choice), on, ALU.mult))
                then(V.tensor_scalar(masked[:, :, :], masked[:, :, :], 0.0, None, ALU.add))

            def choose_experts():
                for i in range(TILES):
                    last = V.max(top8[:, i, :], masked[:, i, :])
                then(last)
                V.memset(spare[:, :], 0.0)
                for i in range(TILES):
                    last = V.match_replace(taken[:, i, :], top8[:, i, :], masked[:, i, :], NEVER)
                then(last)
                then(V.tensor_tensor(chosen[:, :, :], taken[:, :, :], masked[:, :, :], ALU.not_equal))
                then(V.tensor_tensor(chosen[:, :, :], chosen[:, :, :], scores[:, :, :], ALU.mult))

            def weigh_experts():
                then(V.tensor_reduce(w_sum[:, :], chosen[:, :, :], AX.X, ALU.add))
                then(V.tensor_scalar(w_sum[:, :], w_sum[:, :], 1e-20, None, ALU.add))
                then(V.reciprocal(w_sum[:, :], w_sum[:, :]))
                then(V.tensor_scalar(w_sum[:, :], w_sum[:, :], ROUTED_SCALING, None, ALU.mult))
                over = w_sum[:, :].unsqueeze(2).to_broadcast([P, TILES, E])
                for n in range(2):
                    last = V.tensor_tensor(w_row[:, :, n, :], chosen[:, :, :], over, ALU.mult)
                last.then_inc(has_w_row, 1)

            def split_weights(n):
                dve.wait_ge(has_wt_round, n)
                V.scalar_tensor_tensor(wt[:, :], wt_round[:, :].bitcast(F32), const[0:2 * E, C_NEG_W:C_NEG_W + 1],
                                       prep_ps[0:2 * E, :], ALU.mult, ALU.add).then_inc(prep_free, 1)

            def add_output(b):
                dve.wait_ge(prep_full, (b + 1) * PREP_USES + W_EARLY)
                rows = x_rows[:, bass.ds(b * TILES, TILES), :]
                V.tensor_tensor(rows, prep_ps[:, :].rearrange("p (t d) -> p t d", t=TILES), rows, ALU.add).then_inc(prep_free, 1)

            dve.wait_ge(const_in, 16)
            dve.wait_ge(zeroed, 3)
            dve.wait_ge(x_in[0], 16)
            variance(0)
            normalise(0, 1)
            split_inputs(0, 2)
            dve.wait_ge(small_in, 48)
            group_scores(3)
            choose_groups()
            choose_experts()
            weigh_experts()
            steps_each = count[1]
            dve.wait_ge(w_rounded, 1)
            V.tensor_tensor(wg_lo[:, :], wg_raw[:, :], wg_hi[:, :].bitcast(F32), ALU.subtract).then_inc(w_split, 1)
            dve.wait_ge(w_rounded, 2)
            V.tensor_tensor(wu_lo[:, :], wu_raw[:, :], wu_hi[:, :].bitcast(F32), ALU.subtract).then_inc(w_split, 1)
            split_weights(1)
            dve.wait_ge(prep_full, 4)
            dve.sem_inc(prep_free, 1)
            with dve.Fori(0, B // 2) as it:
                for half in range(2):
                    b = it * 2 + half
                    uses = b * PREP_USES + W_EARLY
                    count[0] = (b + 1) * steps_each
                    count[1] = 0
                    for u in range(UNITS):
                        k = half * UNITS + u
                        done = it * (2 * UNITS) + k
                        dve.wait_ge(up_full, done + 1)
                        dve.wait_ge(gate_free, done + 3)
                        if u == 0:
                            dve.wait_ge(weighted_free, done + 1)
                            V.tensor_tensor(weighted[k % 2][:, :], up_ps[k % 2][:, :], silu[k % 2][:, :], ALU.mult).then_inc(up_free, 1)
                        else:
                            V.tensor_tensor(hidden[:, :], up_ps[k % 2][:, :], silu[k % 2][:, :], ALU.mult).then_inc(up_free, 1)
                            pair = b * PAIRS + u - 1
                            dve.wait_ge(up_free, done + 3)
                            dve.wait_ge(spread_full, pair + 1)
                            dve.wait_ge(weighted_free, done + 1)
                            V.tensor_tensor(weighted[k % 2][:, :], spread_ps[(u - 1) % 2][:, :], hidden[:, :], ALU.mult).then_inc(spread_free, 1)
                        if k == UNITS + 1:
                            add_output(it * 2)
                        if u == 2:
                            dve.wait_ge(x_in[1 - half], (it + 1 + half) * 16)
                            variance(b + 1)
                        if u == 3:
                            normalise(b + 1, b + 2)
                        if u == PREP_INPUTS + 1:
                            split_inputs(b + 1, uses + 2)
                        if u == PREP_LOGITS + 1:
                            group_scores(uses + 3)
                        if u == PREP_LOGITS + 2:
                            choose_groups()
                        if u == PREP_LOGITS + 3:
                            choose_experts()
                        if u == PREP_LOGITS + 4:
                            weigh_experts()
                    split_weights(b + 2)
                add_output(it * 2 + 1)
            assert count[1] == steps_each

        @block.tensor
        def _(pe):
            pe.sem_inc(weighted_free, 2)

            def transpose_inputs(n, use):
                pe.wait_ge(has_xn, n)
                pe.wait_ge(prep_free, use + 1)
                for i in range(TILES):
                    last = pe.transpose(prep_ps[:, i * P:(i + 1) * P], xn[:, i, :], ident)
                last.then_inc(prep_full, 1)

            def route(use):
                pe.wait_ge(prep_free, use + 1)
                for i in range(TILES):
                    last = pe.matmul(prep_ps[:, i * E:(i + 1) * E], xt_raw[:, i * P:(i + 1) * P], gate_w[:, :], start=True, stop=True)
                last.then_inc(prep_full, 1)

            def transpose_weights(n, use):
                pe.wait_ge(has_w_row, n)
                pe.wait_ge(prep_free, use + 1)
                for i in range(TILES):
                    last = pe.matmul(prep_ps[0:2 * E, i * P:(i + 1) * P], w_row[:, i, :, :].rearrange("p a e -> p (a e)"), ident, start=True, stop=True)
                last.then_inc(prep_full, 1)

            def transpose_output(b):
                pe.wait_ge(ffn_free, b + 2)
                pe.wait_ge(prep_free, (b + 1) * PREP_USES + W_EARLY)
                for i in range(TILES):
                    last = pe.transpose(prep_ps[:, i * P:(i + 1) * P], ffn_t[:, i * P:(i + 1) * P], ident)
                last.then_inc(prep_full, 1)

            def project(out, hi, lo, u, x_hi, x_lo):
                at = slice(u * P, (u + 1) * P)
                pe.matmul(out[:, :], hi[:, at], x_hi, start=True, stop=False)
                pe.matmul(out[:, :], hi[:, at], x_lo, start=False, stop=False)
                return pe.matmul(out[:, :], lo[:, at], x_hi, start=False, stop=True)

            def down(it, k):
                u = k % UNITS
                done = it * (2 * UNITS) + k
                if u == 0:
                    pe.wait_ge(up_free, done + 3)
                    pe.wait_ge(ffn_free, it * 2 + k // UNITS + 1)
                else:
                    pe.wait_ge(spread_free, (it * 2 + k // UNITS) * PAIRS + u + 2)
                pe.matmul(ffn_ps[:, :], wd[:, u, :], weighted[k % 2][:, :], start=u == 0, stop=u == UNITS - 1).then_inc(weighted_free, 1)

            pe.wait_ge(const_in, 16)
            transpose_inputs(1, 0)
            pe.wait_ge(small_in, 48)
            route(1)
            transpose_weights(1, 2)
            pe.wait_ge(prep_free, 4)
            pe.sem_inc(prep_full, 1)
            pe.wait_ge(w_split, 2)
            pe.wait_ge(picked, 1)
            pe.wait_ge(wd_in, 16)
            with pe.Fori(0, B // 2) as it:
                for half in range(2):
                    b = it * 2 + half
                    uses = b * PREP_USES + W_EARLY
                    x_hi, x_lo = xt_hi[:, bass.ds(b * S, S)], xt_lo[:, bass.ds(b * S, S)]
                    pe.wait_ge(has_xt, b + 1)
                    for u in range(UNITS):
                        k = half * UNITS + u
                        done = it * (2 * UNITS) + k
                        pe.wait_ge(gate_free, done + 1)
                        project(gate_ps[k % 2], wg_hi, wg_lo, u, x_hi, x_lo).then_inc(gate_full, 1)
                        if k:
                            down(it, k - 1)
                        if k == UNITS + 1:
                            transpose_output(it * 2)
                        pe.wait_ge(up_free, done + 1)
                        project(up_ps[k % 2], wu_hi, wu_lo, u, x_hi, x_lo).then_inc(up_full, 1)
                        if u:
                            pair = b * PAIRS + u - 1
                            if u == 1:
                                pe.wait_ge(prep_free, uses)
                            pe.wait_ge(spread_free, pair + 1)
                            pe.matmul(spread_ps[(u - 1) % 2][:, :], pick[:, u - 1, :], wt[:, :], start=True, stop=True).then_inc(spread_full, 1)
                        if u == PREP_INPUTS:
                            transpose_inputs(b + 2, uses)
                        if u == PREP_LOGITS:
                            route(uses + 1)
                        if u == PREP_WEIGHTS:
                            transpose_weights(b + 2, uses + 2)
                down(it, 2 * UNITS - 1)
                transpose_output(it * 2 + 1)


def attention_phase(nc, t, dram):
    with ExitStack() as ctx:
        def sb(name, shape, dt=F32):
            return ctx.enter_context(nc.sbuf_tensor(name, shape, dt))

        def psum(name, shape):
            return ctx.enter_context(nc.psum_tensor(name, shape, F32))

        def sem(name):
            return ctx.enter_context(nc.semaphore(name))

        x_rows, xt_hi, xt_lo, const = t["x_rows"], t["xt_hi"], t["xt_lo"], t["const"]
        ident = const[:, C_IDENT:C_IDENT + P]
        GW = GROUPS * P

        wq_raw, wk_raw = sb("wq_raw", [D, GW]), sb("wk_raw", [D, GW])
        wq = [sb("wq_hi", [D, GW], F32R), sb("wq_lo", [D, GW], F32R)]
        wk = [sb("wk_hi", [D, GW], F32R), sb("wk_lo", [D, GW], F32R)]
        aux_raw = sb("aux_raw", [3, 2, GW])
        aux_const = sb("aux_const", [3, 2, GW])
        aux_sum = sb("aux_sum", [3, 2, GW])
        aux_round = sb("aux_round", [3, 2, GW], F32R)
        aux = sb("aux", [3, 2, GW], F32R)
        aux_rows = sb("aux_rows", [3, S], F32R)
        masks = sb("masks", [P, 2, P], F32R)
        ident_r = sb("ident_r", [P, P], F32R)
        wv_raw = sb("wv_raw", [D, D])
        wv = [sb("wv_hi", [D, D], F32R), sb("wv_lo", [D, D], F32R)]
        wo, bv = sb("wo", [D, D]), sb("bv", [1, D])

        x_seq = [sb("x_seq_hi", [D, S], F32R), sb("x_seq_lo", [D, S], F32R)]
        rounded = sb("rounded", [P, S], F32R)
        q_rows = [sb(f"q_rows{g}", [P, S], F32R) for g in range(GROUPS)]
        k_rows = [sb(f"k_rows{g}", [P, S], F32R) for g in range(GROUPS)]
        qm_rows = [sb(f"qm_rows{g}", [P, S], F32R) for g in range(GROUPS)]
        neg_max = [sb(f"neg_max{n}", [P, TILES, PER]) for n in range(2)]
        max_cols = sb("max_cols", [P, TILES, P], F32R)
        weights = [sb(f"weights{n}", [P, S]) for n in range(2 * PER)]
        values = sb("values", [P, TILES, HEADS, 32])
        sums_t = sb("sums_t", [P, S])
        divisor = sb("divisor", [P, TILES, PER])
        heads_out = sb("heads_out", [P, TILES, D])
        heads_out_t = sb("heads_out_t", [D, S])
        result = sb("result", [P, TILES, D])

        max_ps = [psum(f"max_ps{n}", [P, 2, S]) for n in range(2)]
        score_ps = [psum(f"score_ps{n}", [P, S]) for n in range(2)]
        sums_ps = psum("sums_ps", [P, S])
        misc_ps = psum("misc_ps", [P, S])

        weights_in = sem("weights_in")
        zeroed = sem("zeroed")
        weights_scaled, aux_summed, aux_rounded = sem("weights_scaled"), sem("aux_summed"), sem("aux_rounded")
        weights_rounded, weights_split = sem("weights_rounded"), sem("weights_split")
        ones_set = sem("ones_set")
        seq_in = sem("seq_in")
        misc_full, misc_free = sem("misc_full"), sem("misc_free")
        qk_rounded = sem("qk_rounded")
        max_full, max_free = sem("max_full"), sem("max_free")
        max_high, max_split = sem("max_high"), sem("max_split")
        score_full, score_free = sem("score_full"), sem("score_free")
        weights_free = sem("weights_free")
        sums_moved, sums_turned, divided, has_divisor = sem("sums_moved"), sem("sums_turned"), sem("divided"), sem("has_divisor")
        heads_turned, heads_moved = sem("heads_turned"), sem("heads_moved")
        projected, result_full, result_out = sem("projected"), sem("result_full"), sem("result_out")

        MISC_EARLY, MISC_GROUP, MISC_SEQ = 6, 3, 3 * GROUPS + 1
        QB = [3, 2, 1, 0]

        block = ctx.enter_context(nc.Block())

        @block.sync
        def _(sp):
            for dst, name in ((wq_raw, "wq"), (wk_raw, "wk"), (wv_raw, "wv"), (wo, "wo"), (bv, "bv")):
                sp.dma_start(dst[:, :], dram[name]).then_inc(weights_in, 16)
            sp.dma_start(aux_raw[:, :, :], dram["aux_bias"]).then_inc(weights_in, 16)
            sp.dma_start(aux_const[:, :, :], dram["aux_const"]).then_inc(weights_in, 16)

            def load_sequence(b):
                for dst, src in zip(x_seq, (xt_hi, xt_lo)):
                    sp.dma_start(dst[:, :].bitcast(F32), src[:, bass.ds(b * S, S)].bitcast(F32)).then_inc(seq_in, 16)

            load_sequence(0)
            with sp.Fori(0, B) as b:
                sp.wait_ge(misc_full, b * MISC_SEQ + MISC_EARLY + MISC_GROUP + 2)
                load_sequence(b + 1)
                sp.wait_ge(result_full, b + 2)
                sp.dma_start(dram["out"][:, bass.ds(b * TILES, TILES), :], result[:, :, :]).then_inc(result_out, 16)
            sp.wait_ge(result_out, (B + 1) * 16)
            sp.wait_ge(seq_in, (B + 1) * 32)

        @block.gpsimd
        def _(pool):
            pool.memset(max_cols[:, :, :].bitcast(F32), 0.0).then_inc(zeroed, 1)
            pool.memset(values[:, :, :, :], 0.0).then_inc(zeroed, 1)
            pool.wait_ge(zeroed, 2)
            pool.memset(values[:, :, :, DH:DH + 1], 1.0).then_inc(ones_set, 1)

        @block.scalar
        def _(act):
            act.sem_inc(score_free, 2)
            act.wait_ge(weights_in, 7 * 16)
            act.mul(wq_raw[:, :], wq_raw[:, :], DH ** -0.5).then_inc(weights_scaled, 1)
            act.copy(ident_r[:, :], ident)
            act.copy(masks[:, :, :].rearrange("p a b -> p (a b)"), const[:, C_MASK_Q:C_MASK_Q + 2 * P])
            act.copy(aux_rows[:, :], const[0:3, C_AUX:C_AUX + S])
            act.copy(wk[0][:, :], wk_raw[:, :])
            act.copy(wv[0][:, :], wv_raw[:, :])
            act.wait_ge(weights_scaled, 1)
            act.copy(wq[0][:, :], wq_raw[:, :]).then_inc(weights_rounded, 1)
            act.wait_ge(aux_summed, 1)
            act.copy(aux_round[:, :, :], aux_sum[:, :, :]).then_inc(aux_rounded, 1)

            def round_projection(misc):
                act.wait_ge(misc_full, misc + 1)
                act.copy(rounded[:, :], misc_ps[:, :]).then_inc(qk_rounded, 1)

            def move_values(misc):
                act.wait_ge(misc_full, misc + 1)
                act.copy(values[:, :, :, 0:DH], misc_ps[:, :].rearrange("p (t h d) -> p t h d", t=TILES, d=DH)).then_inc(misc_free, 1)

            for n in range(4):
                round_projection(n)
            act.wait_ge(ones_set, 1)
            move_values(5)
            with act.Fori(0, B) as b:
                misc0 = b * MISC_SEQ + MISC_EARLY
                for g in range(GROUPS):
                    n = b * GROUPS + g
                    misc = misc0 + g * MISC_GROUP
                    for i in range(TILES * PER):
                        kb = i // PER
                        cols = S - kb * P
                        if i % PER == 0:
                            act.wait_ge(weights_free, n * TILES + kb + 1)
                        act.wait_ge(score_full, n * (TILES * PER) + i + 1)
                        act.activation(weights[i % (2 * PER)][:, 0:cols], score_ps[i % 2][:, 0:cols], ACT.Exp).then_inc(score_free, 1)
                        if i == 6:
                            round_projection(misc)
                        if i == 10:
                            round_projection(misc + 1)
                    act.wait_ge(weights_free, (n + 1) * TILES + 2)
                    act.copy(sums_t[:, :], sums_ps[:, :]).then_inc(sums_moved, 1)
                act.wait_ge(heads_turned, b + 1)
                act.copy(heads_out_t[:, :], sums_ps[:, :]).then_inc(heads_moved, 1)
                move_values(misc0 + GROUPS * MISC_GROUP)

        @block.vector
        def _(dve):
            V = nc.vector
            dve.sem_inc(misc_free, 1)
            dve.sem_inc(max_free, 2)
            dve.sem_inc(divided, 1)
            dve.sem_inc(result_full, 1)
            dve.sem_inc(result_out, 16)
            dve.wait_ge(weights_in, 7 * 16)
            V.scalar_tensor_tensor(aux_sum[:, 0, :], aux_raw[:, 0, :], DH ** -0.5, aux_const[:, 0, :], ALU.mult, ALU.add)
            V.tensor_tensor(aux_sum[:, 1, :], aux_raw[:, 1, :], aux_const[:, 1, :], ALU.add).then_inc(aux_summed, 1)
            dve.wait_ge(weights_rounded, 1)
            for raw, (hi, lo) in ((wq_raw, wq), (wk_raw, wk), (wv_raw, wv)):
                V.tensor_tensor(lo[:, :], raw[:, :], hi[:, :].bitcast(F32), ALU.subtract)
            dve.wait_ge(aux_summed, 1)
            dve.wait_ge(aux_rounded, 1)
            V.scalar_tensor_tensor(aux[:, :, :], aux_round[:, :, :].bitcast(F32), const[0:3, C_NEG_AUX:C_NEG_AUX + 1],
                                   aux_sum[:, :, :], ALU.mult, ALU.add).then_inc(weights_split, 1)

            def split_projection(out, neg, n):
                dve.wait_ge(qk_rounded, n + 1)
                V.scalar_tensor_tensor(out[:, :], rounded[:, :].bitcast(F32), const[:, neg:neg + 1],
                                       misc_ps[:, :], ALU.mult, ALU.add).then_inc(misc_free, 1)

            def maximum(g, n, i):
                qb, pair = QB[i // 2], i % 2
                dve.wait_ge(max_full, n * 8 + i + 1)
                V.tensor_reduce(neg_max[g % 2][:, qb, 2 * pair:2 * pair + 2], max_ps[i % 2][:, :, 0:(qb + 1) * P], AX.X, ALU.max, negate=True).then_inc(max_free, 1)

            def split_maxima(g, n):
                cols = max_cols[:, :, :].rearrange("p t (h r) -> p t h r", r=32)
                dve.wait_ge(max_free, n * 8 + 10)
                V.tensor_copy(cols[:, :, :, 28], neg_max[g % 2][:, :, :]).then_inc(max_high, 1)
                dve.wait_ge(max_high, n + 1)
                V.tensor_tensor(cols[:, :, :, 29], neg_max[g % 2][:, :, :], cols[:, :, :, 28].bitcast(F32), ALU.subtract).then_inc(max_split, 1)

            def add_maxima(g, misc):
                dve.wait_ge(misc_full, misc + 1)
                V.tensor_tensor(qm_rows[g][:, :], misc_ps[:, :], q_rows[g][:, :].bitcast(F32), ALU.add).then_inc(misc_free, 1)

            for n in range(4):
                split_projection((q_rows, k_rows)[n % 2][n // 2], (C_NEG_Q, C_NEG_K)[n % 2], n)
            dve.wait_ge(zeroed, 1)
            for i in range(8):
                maximum(0, 0, i)
            split_maxima(0, 0)
            add_maxima(0, 4)
            maximum(1, 1, 0)
            maximum(1, 1, 1)
            with dve.Fori(0, B) as b:
                misc0 = b * MISC_SEQ + MISC_EARLY
                for g in range(GROUPS):
                    n = b * GROUPS + g
                    misc = misc0 + g * MISC_GROUP
                    new = (g + 2) % GROUPS
                    for i in range(2, 8):
                        maximum(g + 1, n + 1, i)
                        if i == 4:
                            split_projection(q_rows[new], C_NEG_Q, n * 2 + 4)
                        if i == 6:
                            split_projection(k_rows[new], C_NEG_K, n * 2 + 5)
                    split_maxima(g + 1, n + 1)
                    maximum(g + 2, n + 2, 0)
                    add_maxima((g + 1) % GROUPS, misc + 2)
                    maximum(g + 2, n + 2, 1)
                    dve.wait_ge(sums_turned, n + 1)
                    turned = sums_ps[:, :].rearrange("p (t h r) -> p t h r", t=TILES, r=32)
                    V.reciprocal(divisor[:, :, :], turned[:, :, :, DH]).then_inc(has_divisor, 1)
                    dve.wait_ge(has_divisor, n + 1)
                    out = heads_out[:, :, g * 32:(g + 1) * 32].rearrange("p t (h d) -> p t h d", d=DH)
                    V.tensor_tensor(out, turned[:, :, :, 0:DH], divisor[:, :, :].unsqueeze(3).to_broadcast([P, TILES, PER, DH]), ALU.mult).then_inc(divided, 1)
                dve.wait_ge(projected, b + 1)
                dve.wait_ge(result_out, (b + 1) * 16)
                V.tensor_tensor(result[:, :, :], sums_ps[:, :].rearrange("p (t d) -> p t d", t=TILES),
                                x_rows[:, bass.ds(b * TILES, TILES), :], ALU.add).then_inc(result_full, 1)

        @block.tensor
        def _(pe):
            pe.sem_inc(weights_free, 2)

            def three_passes(out, lhs, rhs):
                pe.matmul(out, lhs[0], rhs[0], start=True, stop=False)
                pe.matmul(out, lhs[0], rhs[1], start=False, stop=False)
                pe.matmul(out, lhs[1], rhs[0], start=False, stop=False)

            def project(w, which, g, misc):
                at = slice(g * P, (g + 1) * P)
                pe.wait_ge(misc_free, misc + 1)
                three_passes(misc_ps[:, :], [w[0][:, at], w[1][:, at]], [x_seq[0][:, :], x_seq[1][:, :]])
                pe.matmul(misc_ps[:, :], aux[:, which, at], aux_rows[:, :], start=False, stop=True).then_inc(misc_full, 1)

            def score(out, lhs, rhs, head, mask, diagonal):
                rows = slice(32 * head, 32 * head + 32)
                pe.matmul(out, lhs[rows, :], rhs[rows, :], start=True, stop=False)
                return pe.matmul(diagonal, ident_r[:, :], masks[:, mask, :], start=False, stop=True)

            def maxima(g, n, i):
                qb, pair = QB[i // 2], i % 2
                pe.wait_ge(max_free, n * 8 + i + 1)
                keys = (qb + 1) * P
                for j in range(2):
                    out = max_ps[i % 2][:, j, :]
                    last = score(out[:, 0:keys], q_rows[g][:, qb * P:(qb + 1) * P], k_rows[g][:, 0:keys],
                                 2 * pair + j, 0, out[:, qb * P:keys])
                last.then_inc(max_full, 1)

            def turn_maxima(n, misc):
                pe.wait_ge(max_split, n + 1)
                pe.wait_ge(misc_free, misc + 1)
                for i in range(TILES):
                    last = pe.matmul(misc_ps[:, i * P:(i + 1) * P], max_cols[:, i, :], ident_r[:, :], start=True, stop=True)
                last.then_inc(misc_full, 1)

            def project_values(misc):
                pe.wait_ge(misc_free, misc + 1)
                for i in range(TILES):
                    at = slice(i * P, (i + 1) * P)
                    out = misc_ps[:, at]
                    three_passes(out, [x_seq[0][:, at], x_seq[1][:, at]], [wv[0][:, :], wv[1][:, :]])
                    last = pe.matmul(out, const[0:1, C_AUX:C_AUX + P], bv[:, :], start=False, stop=True)
                last.then_inc(misc_full, 1)

            def multiply(g, n, kb):
                pe.wait_ge(score_free, n * (TILES * PER) + (kb + 1) * PER + 2)
                for j in range(PER):
                    last = pe.matmul(sums_ps[32 * j:32 * j + 32, kb * P:], values[:, kb, g * PER + j, :],
                                     weights[(kb * PER + j) % (2 * PER)][:, 0:S - kb * P], start=kb == 0, stop=kb == TILES - 1)
                last.then_inc(weights_free, 1)

            pe.wait_ge(weights_split, 1)
            pe.wait_ge(seq_in, 32)
            for g in range(2):
                project(wq, 0, g, 2 * g)
                project(wk, 1, g, 2 * g + 1)
            pe.wait_ge(misc_free, 3)
            for i in range(8):
                maxima(0, 0, i)
            turn_maxima(0, 4)
            pe.wait_ge(misc_free, 5)
            for i in range(2):
                maxima(1, 1, i)
            project_values(5)
            with pe.Fori(0, B) as b:
                misc0 = b * MISC_SEQ + MISC_EARLY
                for g in range(GROUPS):
                    n = b * GROUPS + g
                    misc = misc0 + g * MISC_GROUP
                    pe.wait_ge(misc_free, misc if g == 0 else misc + 1)
                    for i in range(TILES * PER):
                        kb, j = i // PER, i % PER
                        pe.wait_ge(score_free, n * (TILES * PER) + i + 1)
                        out = score_ps[i % 2][:, 0:S - kb * P]
                        score(out, k_rows[g][:, kb * P:(kb + 1) * P], qm_rows[g][:, kb * P:], j, 1, out[:, 0:P]).then_inc(score_full, 1)
                        if j == 1 and kb:
                            if kb == 1:
                                pe.wait_ge(divided, n + 1)
                                if g == 0:
                                    pe.wait_ge(result_full, b + 1)
                                    pe.wait_ge(misc_free, misc + 1)
                            multiply(g, n, kb - 1)
                        if i % 2 and i < 12:
                            maxima((g + 1) % GROUPS, n + 1, 2 + i // 2)
                        if i == 5:
                            if g == 2:
                                pe.wait_ge(seq_in, (b + 2) * 32)
                            project(wq, 0, (g + 2) % GROUPS, misc)
                        if i == 9:
                            project(wk, 1, (g + 2) % GROUPS, misc + 1)
                    pe.wait_ge(misc_free, misc + 3)
                    maxima((g + 2) % GROUPS, n + 2, 0)
                    maxima((g + 2) % GROUPS, n + 2, 1)
                    multiply(g, n, TILES - 1)
                    turn_maxima(n + 1, misc + 2)
                    pe.wait_ge(sums_moved, n + 1)
                    for i in range(TILES):
                        last = pe.transpose(sums_ps[:, i * P:(i + 1) * P], sums_t[:, i * P:(i + 1) * P], ident)
                    last.then_inc(sums_turned, 1)
                pe.wait_ge(divided, (b + 1) * GROUPS + 1)
                for i in range(TILES):
                    last = pe.transpose(sums_ps[:, i * P:(i + 1) * P], heads_out[:, i, :], ident)
                last.then_inc(heads_turned, 1)
                project_values(misc0 + GROUPS * MISC_GROUP)
                pe.wait_ge(heads_moved, b + 1)
                for i in range(TILES):
                    at = slice(i * P, (i + 1) * P)
                    last = pe.matmul(sums_ps[:, at], heads_out_t[:, at], wo[:, :], start=True, stop=True)
                last.then_inc(projected, 1)


def constants():
    c = np.zeros((P, C_END), np.float32)
    p = np.arange(P)
    c[:, C_IDENT:C_IDENT + P] = np.eye(P)
    c[E:2 * E, C_NEG_W] = -1
    row = p % 32
    c[(row >= 20) & (row < 28), C_NEG_Q] = -1
    c[(row >= 12) & (row < 20), C_NEG_K] = -1
    c[1, C_NEG_AUX] = -1
    c[:, C_RANK:C_RANK + TILES * N_GROUP] = 2 - np.tile(np.arange(N_GROUP), TILES)
    c[:, C_POW:C_POW + TILES] = -0.5
    c[:, C_MASK_Q:C_MASK_Q + P] = np.where(p[None, :] > p[:, None], -1e30, 0)
    c[:, C_MASK_K:C_MASK_K + P] = np.where(p[:, None] > p[None, :], -1e30, 0)
    c[0:2, C_AUX:] = 1
    c[2, C_AUX:] = np.arange(S)
    return c


def attention_constants():
    start = 2 ** (-2 ** (-(np.log2(HEADS) - 3)))
    slopes = np.array([start * start ** i for i in range(HEADS)], np.float32)
    bits = slopes.view(np.uint32)
    high = ((bits + 0x7ff + ((bits >> 12) & 1)) & np.uint32(0xfffff000)).view(np.float32)
    low = slopes - high
    c = np.zeros((3, 2, HEADS, 32), np.float32)
    q, k = c[:, 0], c[:, 1]
    q[0:2, :, 0], q[0:2, :, 2] = high, low
    k[0:2, :, 1], k[0:2, :, 3] = -high, -low
    q[2, :, [1, 3]] = 1
    k[2, :, [0, 2]] = 1
    k[0:2, :, 28:30] = 1
    return c.reshape(3, 2, HEADS * 32)


def program(nc, dram, phases=2):
    with ExitStack() as ctx:
        def sb(name, shape, dt=F32):
            return ctx.enter_context(nc.sbuf_tensor(name, shape, dt))

        t = {
            "x_rows": sb("x_rows", [P, (B + 1) * TILES, D]),
            "xt_hi": sb("xt_hi", [P, (B + 1) * S], F32R),
            "xt_lo": sb("xt_lo", [P, (B + 1) * S], F32R),
            "const": sb("const", [P, C_END]),
        }
        expert_phase(nc, t, dram)
        if phases == 2:
            attention_phase(nc, t, dram)
        else:
            with ExitStack() as c2:
                done = c2.enter_context(nc.semaphore("done"))
                block = c2.enter_context(nc.Block())
                @block.sync
                def _(sp):
                    sp.dma_start(dram["out"], t["x_rows"][:, 0:B * TILES, :]).then_inc(done, 16)
                    sp.wait_ge(done, 16)


def layout(a):
    f = {k: np.asarray(v) for k, v in a.items()}
    pair = lambda w, shared: np.concatenate([shared.T, w.transpose(2, 0, 1).reshape(D, E * I)], axis=1)
    down = f["L0_ffn_expert_down"].transpose(0, 2, 1).reshape(PAIRS, P, D).transpose(1, 0, 2)
    pick = np.zeros((2 * E, PAIRS, P), np.float32)
    for e in range(E):
        pick[[e, E + e], e // 2, (e % 2) * I:(e % 2 + 1) * I] = 1

    def padded(w, starts):
        out = np.zeros((w.shape[0], HEADS, 32), np.float32)
        for at in starts:
            out[:, :, at:at + DH] = w.reshape(-1, HEADS, DH)
        return out.reshape(-1, HEADS * 32)

    aux_bias = np.zeros((3, 2, HEADS * 32), np.float32)
    aux_bias[0:2, 0] = padded(f["L0_attn_bq"].reshape(1, D), (4, 12, 20))
    aux_bias[0:2, 1] = padded(f["L0_attn_bk"].reshape(1, D), (4, 12, 20))
    return {
        "x": f["L0_attn_x"].reshape(B * S, D),
        "const": constants(),
        "gate_w": f["L0_ffn_gate_w"].T,
        "gate_b": np.broadcast_to(f["L0_ffn_gate_bias"], (P, TILES, E)),
        "bo": f["L0_attn_bo"].reshape(D, 1),
        "pick": pick.reshape(2 * E, PAIRS * P),
        "wq": padded(f["L0_attn_Wq"].T, (4, 12, 20)),
        "wk": padded(f["L0_attn_Wk"].T, (4, 12, 20)),
        "wv": f["L0_attn_Wv"].T,
        "wo": f["L0_attn_Wo"].T,
        "bv": f["L0_attn_bv"].reshape(1, D),
        "aux_bias": aux_bias,
        "aux_const": attention_constants(),
        "wg": pair(f["L0_ffn_expert_gate"], f["L0_ffn_shared_gate"]),
        "wu": pair(f["L0_ffn_expert_up"], f["L0_ffn_shared_up"]),
        "wd": np.concatenate([f["L0_ffn_shared_down"].T[:, None, :], down], axis=1),
    }


def build(nc, arrays, phases=2):
    dram = {n: nc.dram_tensor("in_" + n, a.shape, mybir.dt.from_np(a.dtype), kind="ExternalInput").ap() for n, a in arrays.items()}
    dram["x"] = dram["x"].rearrange("(n p) d -> p n d", p=P)
    dram["out"] = nc.dram_tensor("out", (B, S, D), F32, kind="ExternalOutput").ap().rearrange("b (n p) d -> p (b n) d", p=P)
    program(nc, dram, phases)


def kernel(**inputs):
    import concourse.bacc as bacc
    from concourse.bass_utils import run_bass_kernel_spmd

    nc = bacc.Bacc("TRN2", target_bir_lowering=False, num_devices=1)
    arrays = {n: np.ascontiguousarray(a) for n, a in layout(inputs).items()}
    build(nc, arrays)
    r = run_bass_kernel_spmd(nc, [{"in_" + n: a for n, a in arrays.items()}], core_ids=[0])
    return r.results[0]["out"]
```

```python
from contextlib import ExitStack

import numpy as np

import concourse.bass as bass
from concourse import mybir

F32 = mybir.dt.float32
F32R = mybir.dt.float32r
ALU = mybir.AluOpType
ACT = mybir.ActivationFunctionType
AX = mybir.AxisListType

P = 128
B, S, D = 16, 512, 128
TILES = S // P
HEADS, DH = 16, 8
PER, GROUPS = 4, 4
E, I = 32, 64
N_GROUP, TOP_K = 4, 8
PER_GROUP = E // N_GROUP
ROUTED_SCALING = 2.5
EPS = 1e-5
WARM = 40
PAIRS = E // 2
UNITS = PAIRS + 1
NEVER = -3e38
PREP_INPUTS, PREP_LOGITS, PREP_WEIGHTS = 5, 8, 15
FINISH = 3

C_IDENT = 0
C_NEG_W = C_IDENT + P
C_NEG_Q = C_NEG_W + 1
C_NEG_K = C_NEG_Q + 1
C_NEG_AUX = C_NEG_K + 1
C_RANK = C_NEG_AUX + 1
C_POW = C_RANK + TILES * N_GROUP
C_MASK_Q = C_POW + TILES
C_MASK_K = C_MASK_Q + P
C_AUX = C_MASK_K + P
C_END = C_AUX + S


def rows_of(x_rows, b):
    return x_rows[:, bass.ds((b + 1) * TILES, TILES), :]


def expert_phase(nc, t, dram):
    with ExitStack() as ctx:
        def sb(name, shape, dt=F32):
            return ctx.enter_context(nc.sbuf_tensor(name, shape, dt))

        def psum(name, shape):
            return ctx.enter_context(nc.psum_tensor(name, shape, F32))

        def sem(name):
            return ctx.enter_context(nc.semaphore(name))

        x_rows, xt_hi, xt_lo, const = t["x_rows"], t["xt_hi"], t["xt_lo"], t["const"]
        ident = const[:, C_IDENT:C_IDENT + P]
        WIDE = PAIRS * P
        wg_raw, wu_raw = sb("wg_raw", [P, WIDE + P]), sb("wu_raw", [P, WIDE + P])
        wg_hi, wg_lo = sb("wg_hi", [P, WIDE + P], F32R), sb("wg_lo", [P, WIDE + P], F32R)
        wu_hi, wu_lo = sb("wu_hi", [P, WIDE + P], F32R), sb("wu_lo", [P, WIDE + P], F32R)
        wd = sb("wd", [P, UNITS, D])
        gate_w = sb("gate_w", [P, E])
        gate_b = sb("gate_b", [P, TILES, E])
        bo = sb("bo", [P, 1])
        pick_raw = wg_raw[0:2 * E, 0:PAIRS * P]
        pick = sb("pick", [2 * E, PAIRS, P], F32R)

        stats = sb("stats", [P, TILES, 6])
        mean_var = sb("mean_var", [P, TILES, 2])
        var_eps = sb("var_eps", [P, TILES])
        rstd = sb("rstd", [P, TILES])
        xn = sb("xn", [P, TILES, D])
        xt_raw = sb("xt_raw", [P, S])
        th = sb("th", [P, TILES, E])
        scores = sb("scores", [P, TILES, E])
        choice = sb("choice", [P, TILES, E])
        TG = TILES * N_GROUP
        hi1, lo1 = sb("hi1", [P, TG, 4]), sb("lo1", [P, TG, 4])
        hi2, lo2a = sb("hi2", [P, TG, 2]), sb("lo2a", [P, TG, 2])
        lo2b, lo2 = sb("lo2b", [P, TG, 2]), sb("lo2", [P, TG, 2])
        hi3, lo3a = sb("hi3", [P, TG]), sb("lo3a", [P, TG])
        lo3b, lo3 = sb("lo3b", [P, TG]), sb("lo3", [P, TG])
        group_score = sb("group_score", [P, TILES, N_GROUP])
        beats = [sb(f"beats{d}", [P, TILES, N_GROUP + d]) for d in (1, 2, 3)]
        net = [sb(f"net{d}", [P, TILES, N_GROUP]) for d in (1, 2, 3)]
        group_on = sb("group_on", [P, TILES, N_GROUP])
        masked = sb("masked", [P, TILES, E])
        top8 = sb("top8", [P, TILES, TOP_K])
        taken = sb("taken", [P, TILES, E])
        chosen = sb("chosen", [P, TILES, E])
        w_sum = sb("w_sum", [P, TILES])
        spare = sb("spare", [P, 1])
        w_row = sb("w_row", [P, TILES, 2, E])
        wt_round = sb("wt_round", [2 * E, S], F32R)
        wt = sb("wt", [2 * E, S], F32R)

        silu = [sb(f"silu{n}", [P, S]) for n in range(2)]
        hidden = [sb("hidden%d" % i, [P, S]) for i in range(2)]
        weighted = [sb(f"weighted{n}", [P, S]) for n in range(2)]
        ffn_t = sb("ffn_t", [D, S])

        gate_ps = [psum(f"gate_ps{n}", [P, S]) for n in range(2)]
        up_ps = [psum(f"up_ps{n}", [P, S]) for n in range(2)]
        spread_ps = [psum(f"spread_ps{n}", [P, S]) for n in range(2)]
        ffn_ps = psum("ffn_ps", [P, S])
        prep_ps = psum("prep_ps", [P, S])

        x_in = [sem("x_in0"), sem("x_in1")]
        const_in = sem("const_in")
        small_in = sem("small_in")
        pick_in = sem("pick_in")
        wg_in, wu_in, wd_in = sem("wg_in"), sem("wu_in"), sem("wd_in")
        zeroed = sem("zeroed")
        w_rounded = sem("w_rounded")
        w_split = sem("w_split")
        picked = sem("picked")
        has_var, has_rstd, has_xn = sem("has_var"), sem("has_rstd"), sem("has_xn")
        has_xt = sem("has_xt")
        has_w_row = sem("has_w_row")
        has_wt_round = sem("has_wt_round")
        step = sem("step")
        prep_full, prep_free = sem("prep_full"), sem("prep_free")
        gate_full, gate_free = sem("gate_full"), sem("gate_free")
        up_full, up_free = sem("up_full"), sem("up_free")
        spread_full, spread_free = sem("spread_full"), sem("spread_free")
        ffn_free = sem("ffn_free")
        weighted_full, weighted_free = sem("weighted_full"), sem("weighted_free")

        PREP_USES, PREP_EARLY = 4, 3

        block = ctx.enter_context(nc.Block())

        @block.sync
        def _(sp):
            sp.dma_start(const[:, :], dram["const"]).then_inc(const_in, 16)
            for b in range(2):
                sp.dma_start(rows_of(x_rows, b), dram["x"][:, b * TILES:(b + 1) * TILES, :]).then_inc(x_in[b], 16)
            sp.dma_start(gate_w[:, :], dram["gate_w"]).then_inc(small_in, 16)
            sp.dma_start(gate_b[:, :, :], dram["gate_b"]).then_inc(small_in, 16)
            sp.dma_start(bo[:, :], dram["bo"]).then_inc(small_in, 16)
            sp.dma_start(wg_raw[:, :], dram["wg"]).then_inc(wg_in, 16)
            sp.dma_start(wu_raw[:, :], dram["wu"]).then_inc(wu_in, 16)
            sp.dma_start(wd[:, :, :], dram["wd"]).then_inc(wd_in, 16)
            sp.wait_ge(w_split, 1)
            sp.dma_start(pick_raw, dram["pick"]).then_inc(pick_in, 16)
            with sp.Fori(1, B // 2) as it:
                for half in range(2):
                    sp.wait_ge(x_in[half], it * 16)
                    b = it * 2 + half
                    sp.dma_start(rows_of(x_rows, b), dram["x"][:, bass.ds(b * TILES, TILES), :]).then_inc(x_in[half], 16)
            sp.wait_ge(x_in[0], B // 2 * 16)
            sp.dma_start(rows_of(x_rows, B), dram["x"][:, 0:TILES, :]).then_inc(x_in[0], 16)

        @block.gpsimd
        def _(pool):
            for d in range(3):
                pool.memset(beats[d][:, :, :], 0.0).then_inc(zeroed, 1)
            for n in range(2):
                pool.memset(weighted[n][:, :], 0.0).then_inc(zeroed, 1)
            pool.memset(x_rows[:, 0:TILES, :], 0.0).then_inc(zeroed, 1)
            pool.wait_ge(const_in, 16)

            def inverse_deviation(count):
                pool.wait_ge(has_var, count)
                pool.tensor_tensor(rstd[:, :], var_eps[:, :], const[:, C_POW:C_POW + TILES], ALU.pow).then_inc(has_rstd, 1)

            inverse_deviation(1)
            with pool.Fori(0, B) as b:
                inverse_deviation(b + 2)

        @block.scalar
        def _(act):
            act.sem_inc(gate_free, 2)

            def copy_inputs(n, splits):
                if splits is not None:
                    act.wait_ge(has_xt, splits)
                act.wait_ge(prep_full, n)
                act.copy(xt_raw[:, :], prep_ps[:, :]).then_inc(prep_free, 1)

            def gate_tanh(n):
                act.wait_ge(prep_full, n)
                act.activation(th[:, :, :].rearrange("p t e -> p (t e)"), prep_ps[:, 0:TILES * E], ACT.Tanh, scale=0.5).then_inc(prep_free, 1)

            def round_weights(n):
                act.wait_ge(prep_full, n)
                act.copy(wt_round[:, :], prep_ps[0:2 * E, :]).then_inc(has_wt_round, 1)

            copy_inputs(1, None)
            gate_tanh(2)
            act.wait_ge(wg_in, 16)
            act.copy(wg_hi[:, :], wg_raw[:, :]).then_inc(w_rounded, 1)
            act.wait_ge(wu_in, 16)
            act.copy(wu_hi[:, :], wu_raw[:, :]).then_inc(w_rounded, 1)
            act.wait_ge(small_in, 48)
            act.wait_ge(pick_in, 16)
            act.copy(pick[:, :, :].rearrange("p a b -> p (a b)"), pick_raw).then_inc(picked, 1)
            round_weights(3)

            def finish_ffn(b):
                act.wait_ge(weighted_free, (b + 1) * UNITS + 2)
                act.wait_ge(prep_free, (b + 1) * PREP_USES + 1)
                act.activation(ffn_t[:, :], ffn_ps[:, :], ACT.Identity, bias=bo[:, 0:1]).then_inc(ffn_free, 1)

            with act.Fori(0, B // 2) as it:
                for half in range(2):
                    b = it * 2 + half
                    uses = b * PREP_USES + PREP_EARLY
                    for u in range(UNITS):
                        k = half * UNITS + u
                        done = it * (2 * UNITS) + k
                        act.wait_ge(gate_full, done + 1)
                        act.wait_ge(up_free, done + 1)
                        act.activation(silu[k % 2][:, :], gate_ps[k % 2][:, :], ACT.Silu).then_inc(gate_free, 1)
                        if u == 1:
                            finish_ffn(b - 1)
                        if u == PREP_INPUTS:
                            copy_inputs(uses + 2, b + 1)
                        if u == PREP_LOGITS:
                            gate_tanh(uses + 3)
                        if u == PREP_WEIGHTS:
                            round_weights(uses + 4)
            finish_ffn(B - 1)

        @block.vector
        def _(dve):
            V = nc.vector
            dve.sem_inc(prep_free, 1)
            dve.sem_inc(up_free, 2)
            dve.sem_inc(spread_free, 2)
            count = [0, 0]

            def then(instruction):
                instruction.then_inc(step, 1)
                count[1] += 1
                dve.wait_ge(step, count[0] + count[1])

            def variance(b):
                rows = rows_of(x_rows, b)
                for i in range(TILES):
                    last = V.bn_stats(stats[:, i, :], rows[:, i, :])
                then(last)
                V.memset(spare[:, :], 0.0)
                for i in range(TILES):
                    last = V.bn_aggr(mean_var[:, i, :], stats[:, i, :])
                then(last)
                V.tensor_scalar(var_eps[:, :], mean_var[:, :, 1], EPS, None, ALU.add).then_inc(has_var, 1)

            def normalise(b, n):
                rows = rows_of(x_rows, b)
                dve.wait_ge(has_rstd, n)
                for i in range(TILES):
                    last = V.tensor_scalar(xn[:, i, :], rows[:, i, :], mean_var[:, i, 0:1], rstd[:, i:i + 1], ALU.subtract, ALU.mult)
                last.then_inc(has_xn, 1)

            def split_inputs(b, n):
                dve.wait_ge(prep_free, n)
                at = bass.ds(b * S, S)
                then(V.tensor_copy(xt_hi[:, at], xt_raw[:, :]))
                V.tensor_tensor(xt_lo[:, at], xt_raw[:, :], xt_hi[:, at].bitcast(F32), ALU.subtract).then_inc(has_xt, 1)

            def grp(a):
                return a[:, :, :].rearrange("p t (g e) -> p (t g) e", g=N_GROUP)

            def group_scores(n):
                dve.wait_ge(prep_free, n)
                then(V.tensor_scalar(scores[:, :, :], th[:, :, :], 0.5, 0.5, ALU.mult, ALU.add))
                then(V.tensor_tensor(choice[:, :, :], scores[:, :, :], gate_b[:, :, :], ALU.add))
                c = grp(choice)
                V.tensor_tensor(hi1[:, :, :], c[:, :, 0:4], c[:, :, 4:8], ALU.max)
                then(V.tensor_tensor(lo1[:, :, :], c[:, :, 0:4], c[:, :, 4:8], ALU.min))
                V.tensor_tensor(hi2[:, :, :], hi1[:, :, 0:2], hi1[:, :, 2:4], ALU.max)
                V.tensor_tensor(lo2a[:, :, :], hi1[:, :, 0:2], hi1[:, :, 2:4], ALU.min)
                then(V.tensor_tensor(lo2b[:, :, :], lo1[:, :, 0:2], lo1[:, :, 2:4], ALU.max))
                then(V.tensor_tensor(lo2[:, :, :], lo2a[:, :, :], lo2b[:, :, :], ALU.max))
                V.tensor_tensor(hi3[:, :], hi2[:, :, 0], hi2[:, :, 1], ALU.max)
                V.tensor_tensor(lo3a[:, :], hi2[:, :, 0], hi2[:, :, 1], ALU.min)
                then(V.tensor_tensor(lo3b[:, :], lo2[:, :, 0], lo2[:, :, 1], ALU.max))
                then(V.tensor_tensor(lo3[:, :], lo3a[:, :], lo3b[:, :], ALU.max))
                then(V.tensor_tensor(group_score[:, :, :].rearrange("p t g -> p (t g)"), hi3[:, :], lo3[:, :], ALU.add))

            def choose_groups():
                g = group_score
                for d in (1, 2, 3):
                    last = V.tensor_tensor(beats[d - 1][:, :, d:N_GROUP], g[:, :, 0:N_GROUP - d], g[:, :, d:N_GROUP], ALU.is_ge)
                then(last)
                for d in (1, 2, 3):
                    last = V.tensor_tensor(net[d - 1][:, :, :], beats[d - 1][:, :, d:N_GROUP + d], beats[d - 1][:, :, 0:N_GROUP], ALU.subtract)
                then(last)
                then(V.tensor_tensor(net[0][:, :, :], net[0][:, :, :], net[1][:, :, :], ALU.add))
                then(V.tensor_tensor(net[0][:, :, :], net[0][:, :, :], net[2][:, :, :], ALU.add))
                rank = const[:, C_RANK:C_RANK + TG].rearrange("p (t g) -> p t g", t=TILES)
                then(V.tensor_tensor(group_on[:, :, :], net[0][:, :, :], rank, ALU.is_ge))
                on = group_on[:, :, :].rearrange("p t g -> p (t g)").unsqueeze(2).to_broadcast([P, TG, PER_GROUP])
                then(V.tensor_tensor(grp(masked), grp(choice), on, ALU.mult))
                then(V.tensor_scalar(masked[:, :, :], masked[:, :, :], 0.0, None, ALU.add))

            def choose_experts():
                for i in range(TILES):
                    last = V.max(top8[:, i, :], masked[:, i, :])
                then(last)
                V.memset(spare[:, :], 0.0)
                for i in range(TILES):
                    last = V.match_replace(taken[:, i, :], top8[:, i, :], masked[:, i, :], NEVER)
                then(last)
                then(V.tensor_tensor(chosen[:, :, :], taken[:, :, :], masked[:, :, :], ALU.not_equal))
                then(V.tensor_tensor(chosen[:, :, :], chosen[:, :, :], scores[:, :, :], ALU.mult))

            def weigh_experts():
                then(V.tensor_reduce(w_sum[:, :], chosen[:, :, :], AX.X, ALU.add))
                then(V.tensor_scalar(w_sum[:, :], w_sum[:, :], 1e-20, None, ALU.add))
                then(V.reciprocal(w_sum[:, :], w_sum[:, :]))
                then(V.tensor_scalar(w_sum[:, :], w_sum[:, :], ROUTED_SCALING, None, ALU.mult))
                over = w_sum[:, :].unsqueeze(2).to_broadcast([P, TILES, E])
                for n in range(2):
                    last = V.tensor_tensor(w_row[:, :, n, :], chosen[:, :, :], over, ALU.mult)
                last.then_inc(has_w_row, 1)

            def split_weights(n):
                dve.wait_ge(has_wt_round, n)
                V.scalar_tensor_tensor(wt[:, :], wt_round[:, :].bitcast(F32), const[0:2 * E, C_NEG_W:C_NEG_W + 1],
                                       prep_ps[0:2 * E, :], ALU.mult, ALU.add).then_inc(prep_free, 1)

            def add_output(b):
                dve.wait_ge(prep_full, (b + 1) * PREP_USES + PREP_EARLY + 1)
                rows = rows_of(x_rows, b)
                V.tensor_tensor(rows, prep_ps[:, :].rearrange("p (t d) -> p t d", t=TILES), rows, ALU.add).then_inc(prep_free, 1)

            dve.wait_ge(const_in, 16)
            dve.wait_ge(zeroed, 6)
            dve.wait_ge(x_in[0], 16)
            variance(0)
            normalise(0, 1)
            split_inputs(0, 2)
            dve.wait_ge(small_in, 48)
            group_scores(3)
            choose_groups()
            choose_experts()
            weigh_experts()
            steps_each = count[1]
            dve.wait_ge(w_rounded, 1)
            V.tensor_tensor(wg_lo[:, :], wg_raw[:, :], wg_hi[:, :].bitcast(F32), ALU.subtract).then_inc(w_split, 1)
            dve.wait_ge(w_rounded, 2)
            V.tensor_tensor(wu_lo[:, :], wu_raw[:, :], wu_hi[:, :].bitcast(F32), ALU.subtract).then_inc(w_split, 1)
            split_weights(1)
            with dve.Fori(0, B // 2) as it:
                for half in range(2):
                    b = it * 2 + half
                    uses = b * PREP_USES + PREP_EARLY
                    count[0] = (b + 1) * steps_each
                    count[1] = 0
                    for u in range(UNITS):
                        k = half * UNITS + u
                        done = it * (2 * UNITS) + k
                        dve.wait_ge(up_full, done + 1)
                        dve.wait_ge(gate_free, done + 3)
                        if u == 0:
                            dve.wait_ge(weighted_free, done + 1)
                            V.tensor_tensor(weighted[k % 2][:, :], up_ps[k % 2][:, :], silu[k % 2][:, :], ALU.mult).then_inc(up_free, 1)
                        else:
                            V.tensor_tensor(hidden[k % 2][:, :], up_ps[k % 2][:, :], silu[k % 2][:, :], ALU.mult).then_inc(up_free, 1)
                            pair = b * PAIRS + u - 1
                            dve.wait_ge(up_free, done + 3)
                            dve.wait_ge(spread_full, pair + 1)
                            dve.wait_ge(weighted_free, done + 1)
                            V.tensor_tensor(weighted[k % 2][:, :], spread_ps[(u - 1) % 2][:, :], hidden[k % 2][:, :], ALU.mult).then_inc(spread_free, 1)
                        if u == FINISH:
                            add_output(b - 1)
                        if u == 2:
                            dve.wait_ge(x_in[1 - half], (it + 1 + half) * 16)
                            variance(b + 1)
                        if u == 3:
                            normalise(b + 1, b + 2)
                        if u == PREP_INPUTS + 1:
                            split_inputs(b + 1, uses + 3)
                        if u == PREP_LOGITS + 1:
                            group_scores(uses + 4)
                        if u == PREP_LOGITS + 2:
                            choose_groups()
                        if u == PREP_LOGITS + 3:
                            choose_experts()
                        if u == PREP_LOGITS + 4:
                            weigh_experts()
                    split_weights(b + 2)
            add_output(B - 1)
            assert count[1] == steps_each

        @block.tensor
        def _(pe):
            def transpose_inputs(n, use):
                pe.wait_ge(has_xn, n)
                pe.wait_ge(prep_free, use + 1)
                for i in range(TILES):
                    last = pe.transpose(prep_ps[:, i * P:(i + 1) * P], xn[:, i, :], ident)
                last.then_inc(prep_full, 1)

            def route(use):
                pe.wait_ge(prep_free, use + 1)
                for i in range(TILES):
                    last = pe.matmul(prep_ps[:, i * E:(i + 1) * E], xt_raw[:, i * P:(i + 1) * P], gate_w[:, :], start=True, stop=True)
                last.then_inc(prep_full, 1)

            def transpose_weights(n, use):
                pe.wait_ge(has_w_row, n)
                pe.wait_ge(prep_free, use + 1)
                for i in range(TILES):
                    last = pe.matmul(prep_ps[0:2 * E, i * P:(i + 1) * P], w_row[:, i, :, :].rearrange("p a e -> p (a e)"), ident, start=True, stop=True)
                last.then_inc(prep_full, 1)

            def transpose_output(b):
                pe.wait_ge(ffn_free, b + 2)
                pe.wait_ge(prep_free, (b + 1) * PREP_USES + PREP_EARLY + 1)
                for i in range(TILES):
                    last = pe.transpose(prep_ps[:, i * P:(i + 1) * P], ffn_t[:, i * P:(i + 1) * P], ident)
                last.then_inc(prep_full, 1)

            def project(out, hi, lo, u, x_hi, x_lo):
                at = slice(u * P, (u + 1) * P)
                pe.matmul(out[:, :], hi[:, at], x_hi, start=True, stop=False)
                pe.matmul(out[:, :], hi[:, at], x_lo, start=False, stop=False)
                return pe.matmul(out[:, :], lo[:, at], x_hi, start=False, stop=True)

            def down(b, u, slot):
                if u == 0:
                    pe.wait_ge(up_free, b * UNITS + 3)
                    pe.wait_ge(ffn_free, b + 1)
                else:
                    pe.wait_ge(spread_free, b * PAIRS + u + 2)
                pe.matmul(ffn_ps[:, :], wd[:, u, :], weighted[slot][:, :], start=u == 0, stop=u == UNITS - 1).then_inc(weighted_free, 1)

            pe.wait_ge(const_in, 16)
            transpose_inputs(1, 0)
            pe.wait_ge(small_in, 48)
            route(1)
            transpose_weights(1, 2)
            pe.wait_ge(w_split, 2)
            pe.wait_ge(picked, 1)
            pe.wait_ge(wd_in, 16)
            pe.wait_ge(zeroed, 6)
            pe.matmul(ffn_ps[:, :], wd[:, 0, :], weighted[0][:, :], start=True, stop=False)
            with pe.Fori(0, B // 2) as it:
                for half in range(2):
                    b = it * 2 + half
                    uses = b * PREP_USES + PREP_EARLY
                    x_hi, x_lo = xt_hi[:, bass.ds(b * S, S)], xt_lo[:, bass.ds(b * S, S)]
                    pe.wait_ge(has_xt, b + 1)
                    for u in range(UNITS):
                        k = half * UNITS + u
                        done = it * (2 * UNITS) + k
                        pe.wait_ge(gate_free, done + 1)
                        project(gate_ps[k % 2], wg_hi, wg_lo, u, x_hi, x_lo).then_inc(gate_full, 1)
                        if u < 2:
                            down(b - 1, UNITS - 2 + u, k % 2)
                        else:
                            down(b, u - 2, k % 2)
                        if u == FINISH:
                            transpose_output(b - 1)
                        pe.wait_ge(up_free, done + 1)
                        project(up_ps[k % 2], wu_hi, wu_lo, u, x_hi, x_lo).then_inc(up_full, 1)
                        if u:
                            pair = b * PAIRS + u - 1
                            if u == 1:
                                pe.wait_ge(prep_free, uses + 1)
                            pe.wait_ge(spread_free, pair + 1)
                            pe.matmul(spread_ps[(u - 1) % 2][:, :], pick[:, u - 1, :], wt[:, :], start=True, stop=True).then_inc(spread_full, 1)
                        if u == PREP_INPUTS:
                            transpose_inputs(b + 2, uses + 1)
                        if u == PREP_LOGITS:
                            route(uses + 2)
                        if u == PREP_WEIGHTS:
                            transpose_weights(b + 2, uses + 3)
            down(B - 1, UNITS - 2, 0)
            down(B - 1, UNITS - 1, 1)
            transpose_output(B - 1)


def attention_phase(nc, t, dram):
    with ExitStack() as ctx:
        def sb(name, shape, dt=F32):
            return ctx.enter_context(nc.sbuf_tensor(name, shape, dt))

        def psum(name, shape):
            return ctx.enter_context(nc.psum_tensor(name, shape, F32))

        def sem(name):
            return ctx.enter_context(nc.semaphore(name))

        x_rows, xt_hi, xt_lo, const = t["x_rows"], t["xt_hi"], t["xt_lo"], t["const"]
        ident = const[:, C_IDENT:C_IDENT + P]
        GW = GROUPS * P

        weights = sb("weights", [P, 2 * PER, S])
        wq_raw, wk_raw, wv_raw = weights[:, 0, :], weights[:, 1, :], weights[:, 2, 0:D]
        aux_raw, aux_const = weights[0:3, 4:6, :], weights[0:3, 6:8, :]
        wq = [sb("wq_hi", [D, GW], F32R), sb("wq_lo", [D, GW], F32R)]
        wk = [sb("wk_hi", [D, GW], F32R), sb("wk_lo", [D, GW], F32R)]
        aux = sb("aux", [3, 2, GW], F32R)
        aux_rows = sb("aux_rows", [3, S], F32R)
        masks = sb("masks", [P, 2, P], F32R)
        ident_r = sb("ident_r", [P, P], F32R)
        wv = [sb("wv_hi", [D, D], F32R), sb("wv_lo", [D, D], F32R)]
        wo, bv = sb("wo", [D, D]), sb("bv", [1, D])

        x_seq = [sb("x_seq_hi", [D, S], F32R), sb("x_seq_lo", [D, S], F32R)]
        rounded = sb("rounded", [P, S], F32R)
        q_rows = [sb(f"q_rows{g}", [P, S], F32R) for g in range(2)]
        qm_rows = [sb(f"qm_rows{g}", [P, S], F32R) for g in range(2)]
        k_rows = [sb(f"k_rows{g}", [P, S], F32R) for g in range(2)]
        k_apart = [sb(f"k_apart{g}", [P, PER, S], F32R) for g in range(GROUPS)]
        neg_max = [sb(f"neg_max{n}", [P, TILES, PER]) for n in range(2)]
        max_cols = sb("max_cols", [P, TILES, P], F32R)
        values = sb("values", [P, TILES, HEADS, 32])
        sums_t = sb("sums_t", [P, S])
        divisor = sb("divisor", [P, TILES, PER])
        heads_out = sb("heads_out", [P, TILES, D])
        heads_out_t = sums_t
        result = sb("result", [P, TILES, D])

        max_ps = [psum(f"max_ps{n}", [P, 2, S]) for n in range(2)]
        score_ps = [psum(f"score_ps{n}", [P, S]) for n in range(2)]
        sums_ps = psum("sums_ps", [P, S])
        misc_ps = psum("misc_ps", [P, S])

        weights_in = sem("weights_in")
        zeroed = sem("zeroed")
        weights_scaled, aux_summed, aux_rounded = sem("weights_scaled"), sem("aux_summed"), sem("aux_rounded")
        weights_rounded, weights_split = sem("weights_rounded"), sem("weights_split")
        ones_set = sem("ones_set")
        seq_in = sem("seq_in")
        misc_full, misc_free = sem("misc_full"), sem("misc_free")
        qk_rounded = sem("qk_rounded")
        first_apart, last_apart = sem("first_apart"), sem("last_apart")
        max_full, max_free = sem("max_full"), sem("max_free")
        max_high, max_split = sem("max_high"), sem("max_split")
        score_full, score_free = sem("score_full"), sem("score_free")
        weights_free = sem("weights_free")
        sums_moved, sums_turned, divided, has_divisor = sem("sums_moved"), sem("sums_turned"), sem("divided"), sem("has_divisor")
        heads_turned, heads_moved = sem("heads_turned"), sem("heads_moved")
        projected, result_full, result_out = sem("projected"), sem("result_full"), sem("result_out")

        MISC_EARLY, MISC_GROUP, MISC_SEQ = 6, 3, 3 * GROUPS + 1
        QB = [3, 2, 1, 0]

        block = ctx.enter_context(nc.Block())

        @block.sync
        def _(sp):
            for dst, name in ((wq_raw, "wq"), (wk_raw, "wk"), (wv_raw, "wv"), (wo[:, :], "wo"), (bv[:, :], "bv"),
                              (aux_raw, "aux_bias"), (aux_const, "aux_const")):
                sp.dma_start(dst, dram[name]).then_inc(weights_in, 16)

            def load_sequence(b):
                for dst, src in zip(x_seq, (xt_hi, xt_lo)):
                    sp.dma_start(dst[:, :].bitcast(F32), src[:, bass.ds(b * S, S)].bitcast(F32)).then_inc(seq_in, 16)

            load_sequence(0)
            with sp.Fori(0, B) as b:
                sp.wait_ge(misc_full, b * MISC_SEQ + MISC_EARLY + MISC_GROUP + 2)
                load_sequence(b + 1)
                sp.wait_ge(result_full, b + 2)
                sp.dma_start(dram["out"][:, bass.ds(b * TILES, TILES), :], result[:, :, :]).then_inc(result_out, 16)
            sp.wait_ge(result_out, (B + 1) * 16)
            sp.wait_ge(seq_in, (B + 1) * 32)

        @block.gpsimd
        def _(pool):
            pool.memset(max_cols[:, :, :].bitcast(F32), 0.0).then_inc(zeroed, 1)
            pool.memset(values[:, :, :, :], 0.0).then_inc(zeroed, 1)
            pool.wait_ge(zeroed, 2)
            pool.memset(values[:, :, :, DH:DH + 1], 1.0).then_inc(ones_set, 1)
            for g in range(GROUPS):
                pool.memset(k_apart[g][:, :, :].bitcast(F32), 0.0).then_inc(zeroed, 1)

        @block.scalar
        def _(act):
            act.sem_inc(score_free, 2)
            act.wait_ge(weights_in, 7 * 16)
            act.mul(wq_raw, wq_raw, DH ** -0.5).then_inc(weights_scaled, 1)
            act.copy(ident_r[:, :], ident)
            act.copy(masks[:, :, :].rearrange("p a b -> p (a b)"), const[:, C_MASK_Q:C_MASK_Q + 2 * P])
            act.copy(aux_rows[:, :], const[0:3, C_AUX:C_AUX + S])
            act.copy(wk[0][:, :], wk_raw)
            act.copy(wv[0][:, :], wv_raw)
            act.wait_ge(weights_scaled, 1)
            act.copy(wq[0][:, :], wq_raw).then_inc(weights_rounded, 1)
            act.wait_ge(aux_summed, 1)
            act.copy(aux[:, :, :], aux_const).then_inc(aux_rounded, 1)

            def round_projection(misc):
                act.wait_ge(misc_full, misc + 1)
                act.copy(rounded[:, :], misc_ps[:, :]).then_inc(qk_rounded, 1)

            def move_values(misc):
                act.wait_ge(misc_full, misc + 1)
                act.copy(values[:, :, :, 0:DH], misc_ps[:, :].rearrange("p (t h d) -> p t h d", t=TILES, d=DH)).then_inc(misc_free, 1)

            def set_apart(g, split):
                act.wait_ge(misc_free, split)
                for j in (2, 3):
                    rows = slice(32 * j, 32 * j + 32)
                    last = act.copy(k_apart[g][rows, j, :], k_rows[g % 2][rows, :].bitcast(F32))
                last.then_inc(last_apart, 1)

            act.wait_ge(ones_set, 1)
            act.wait_ge(zeroed, 6)
            for n in range(4):
                round_projection(n)
                if n % 2:
                    set_apart(n // 2, n + 1)
            move_values(5)
            with act.Fori(0, B) as b:
                misc0 = b * MISC_SEQ + MISC_EARLY
                for g in range(GROUPS):
                    n = b * GROUPS + g
                    misc = misc0 + g * MISC_GROUP
                    for i in range(TILES * PER):
                        kb = i // PER
                        cols = S - kb * P
                        if i % PER == 0:
                            act.wait_ge(weights_free, n * TILES + kb + 1)
                        act.wait_ge(score_full, n * (TILES * PER) + i + 1)
                        act.activation(weights[:, i % (2 * PER), 0:cols], score_ps[i % 2][:, 0:cols], ACT.Exp).then_inc(score_free, 1)
                        if i == 4:
                            round_projection(misc)
                        if i == 6:
                            set_apart((g + 2) % GROUPS, misc + 2)
                        if i == 8:
                            round_projection(misc + 1)
                    act.wait_ge(weights_free, (n + 1) * TILES + 2)
                    act.copy(sums_t[:, :], sums_ps[:, :]).then_inc(sums_moved, 1)
                act.wait_ge(heads_turned, b + 1)
                act.copy(heads_out_t[:, :], sums_ps[:, :]).then_inc(heads_moved, 1)
                move_values(misc0 + GROUPS * MISC_GROUP)

        @block.vector
        def _(dve):
            V = nc.vector
            dve.sem_inc(misc_free, 1)
            dve.sem_inc(max_free, 2)
            dve.sem_inc(divided, 1)
            dve.sem_inc(result_full, 1)
            dve.sem_inc(result_out, 16)
            dve.wait_ge(weights_in, 7 * 16)
            V.scalar_tensor_tensor(aux_const[:, 0, :], aux_raw[:, 0, :], DH ** -0.5, aux_const[:, 0, :], ALU.mult, ALU.add)
            V.tensor_tensor(aux_const[:, 1, :], aux_raw[:, 1, :], aux_const[:, 1, :], ALU.add).then_inc(aux_summed, 1)
            dve.wait_ge(weights_rounded, 1)
            for raw, (hi, lo) in ((wq_raw, wq), (wk_raw, wk), (wv_raw, wv)):
                V.tensor_tensor(lo[:, :], raw, hi[:, :].bitcast(F32), ALU.subtract)
            dve.wait_ge(aux_summed, 1)
            dve.wait_ge(aux_rounded, 1)
            V.scalar_tensor_tensor(aux[:, :, :], aux[:, :, :].bitcast(F32), const[0:3, C_NEG_AUX:C_NEG_AUX + 1],
                                   aux_const, ALU.mult, ALU.add).then_inc(weights_split, 1)

            def split_projection(out, neg, n):
                dve.wait_ge(qk_rounded, n + 1)
                V.scalar_tensor_tensor(out[:, :], rounded[:, :].bitcast(F32), const[:, neg:neg + 1],
                                       misc_ps[:, :], ALU.mult, ALU.add).then_inc(misc_free, 1)

            def maximum(g, n, i):
                qb, pair = QB[i // 2], i % 2
                dve.wait_ge(max_full, n * 8 + i + 1)
                V.tensor_reduce(neg_max[g % 2][:, qb, 2 * pair:2 * pair + 2], max_ps[i % 2][:, :, 0:(qb + 1) * P], AX.X, ALU.max, negate=True).then_inc(max_free, 1)

            def split_maxima(g, n):
                cols = max_cols[:, :, :].rearrange("p t (h r) -> p t h r", r=32)
                dve.wait_ge(max_free, n * 8 + 10)
                V.tensor_copy(cols[:, :, :, 28], neg_max[g % 2][:, :, :]).then_inc(max_high, 1)
                dve.wait_ge(max_high, n + 1)
                V.tensor_tensor(cols[:, :, :, 29], neg_max[g % 2][:, :, :], cols[:, :, :, 28].bitcast(F32), ALU.subtract).then_inc(max_split, 1)

            def add_maxima(g, misc):
                dve.wait_ge(misc_full, misc + 1)
                V.tensor_tensor(qm_rows[g % 2][:, :], misc_ps[:, :], q_rows[g % 2][:, :].bitcast(F32), ALU.add).then_inc(misc_free, 1)

            def set_apart(g, split):
                dve.wait_ge(misc_free, split)
                for j in (0, 1):
                    rows = slice(32 * j, 32 * j + 32)
                    last = V.tensor_copy(k_apart[g][rows, j, :], k_rows[g % 2][rows, :].bitcast(F32))
                last.then_inc(first_apart, 1)

            dve.wait_ge(zeroed, 6)
            for n in range(4):
                split_projection((k_rows, q_rows)[n % 2][n // 2], (C_NEG_K, C_NEG_Q)[n % 2], n)
                if n % 2 == 0:
                    set_apart(n // 2, n + 2)
            for i in range(8):
                maximum(0, 0, i)
            split_maxima(0, 0)
            add_maxima(0, 4)
            maximum(1, 1, 0)
            maximum(1, 1, 1)
            with dve.Fori(0, B) as b:
                misc0 = b * MISC_SEQ + MISC_EARLY
                for g in range(GROUPS):
                    n = b * GROUPS + g
                    misc = misc0 + g * MISC_GROUP
                    new = g % 2
                    for i in range(2, 8):
                        maximum(g + 1, n + 1, i)
                        if i == 3:
                            dve.wait_ge(first_apart, n + 1)
                            dve.wait_ge(last_apart, n + 1)
                            split_projection(k_rows[new], C_NEG_K, n * 2 + 4)
                        if i == 4:
                            set_apart((g + 2) % GROUPS, misc + 2)
                        if i == 5:
                            split_projection(q_rows[new], C_NEG_Q, n * 2 + 5)
                    split_maxima(g + 1, n + 1)
                    maximum(g + 2, n + 2, 0)
                    add_maxima((g + 1) % GROUPS, misc + 2)
                    maximum(g + 2, n + 2, 1)
                    dve.wait_ge(sums_turned, n + 1)
                    turned = sums_ps[:, :].rearrange("p (t h r) -> p t h r", t=TILES, r=32)
                    V.reciprocal(divisor[:, :, :], turned[:, :, :, DH]).then_inc(has_divisor, 1)
                    dve.wait_ge(has_divisor, n + 1)
                    out = heads_out[:, :, g * 32:(g + 1) * 32].rearrange("p t (h d) -> p t h d", d=DH)
                    V.tensor_tensor(out, turned[:, :, :, 0:DH], divisor[:, :, :].unsqueeze(3).to_broadcast([P, TILES, PER, DH]), ALU.mult).then_inc(divided, 1)
                dve.wait_ge(projected, b + 1)
                dve.wait_ge(result_out, (b + 1) * 16)
                V.tensor_tensor(result[:, :, :], sums_ps[:, :].rearrange("p (t d) -> p t d", t=TILES),
                                rows_of(x_rows, b), ALU.add).then_inc(result_full, 1)

        @block.tensor
        def _(pe):
            pe.sem_inc(weights_free, 2)

            def three_passes(out, lhs, rhs):
                pe.matmul(out, lhs[0], rhs[0], start=True, stop=False)
                pe.matmul(out, lhs[0], rhs[1], start=False, stop=False)
                pe.matmul(out, lhs[1], rhs[0], start=False, stop=False)

            def project(w, which, g, misc):
                at = slice(g * P, (g + 1) * P)
                pe.wait_ge(misc_free, misc + 1)
                three_passes(misc_ps[:, :], [w[0][:, at], w[1][:, at]], [x_seq[0][:, :], x_seq[1][:, :]])
                pe.matmul(misc_ps[:, :], aux[:, which, at], aux_rows[:, :], start=False, stop=True).then_inc(misc_full, 1)

            def score(out, lhs, rhs, mask, diagonal):
                pe.matmul(out, lhs, rhs, start=True, stop=False)
                return pe.matmul(diagonal, ident_r[:, :], masks[:, mask, :], start=False, stop=True)

            def maxima(g, n, i):
                qb, pair = QB[i // 2], i % 2
                pe.wait_ge(max_free, n * 8 + i + 1)
                keys = (qb + 1) * P
                for j in range(2):
                    out = max_ps[i % 2][:, j, :]
                    last = score(out[:, 0:keys], q_rows[g % 2][:, qb * P:(qb + 1) * P], k_apart[g][:, 2 * pair + j, 0:keys],
                                 0, out[:, qb * P:keys])
                last.then_inc(max_full, 1)

            def turn_maxima(n, misc):
                pe.wait_ge(max_split, n + 1)
                pe.wait_ge(misc_free, misc + 1)
                for i in range(TILES):
                    last = pe.matmul(misc_ps[:, i * P:(i + 1) * P], max_cols[:, i, :], ident_r[:, :], start=True, stop=True)
                last.then_inc(misc_full, 1)

            def project_values(misc):
                pe.wait_ge(misc_free, misc + 1)
                for i in range(TILES):
                    at = slice(i * P, (i + 1) * P)
                    out = misc_ps[:, at]
                    three_passes(out, [x_seq[0][:, at], x_seq[1][:, at]], [wv[0][:, :], wv[1][:, :]])
                    last = pe.matmul(out, const[0:1, C_AUX:C_AUX + P], bv[:, :], start=False, stop=True)
                last.then_inc(misc_full, 1)

            def multiply(g, n, kb):
                pe.wait_ge(score_free, n * (TILES * PER) + (kb + 1) * PER + 2)
                for j in range(PER):
                    last = pe.matmul(sums_ps[32 * j:32 * j + 32, kb * P:], values[:, kb, g * PER + j, :],
                                     weights[:, (kb * PER + j) % (2 * PER), 0:S - kb * P], start=kb == 0, stop=kb == TILES - 1)
                last.then_inc(weights_free, 1)

            for _ in range(WARM):
                pe.matmul(misc_ps[:, :], xt_hi[:, 0:P], xt_hi[:, 0:S], start=True, stop=True)
            pe.wait_ge(weights_split, 1)
            pe.wait_ge(seq_in, 32)
            for g in range(2):
                project(wk, 1, g, 2 * g)
                project(wq, 0, g, 2 * g + 1)
            pe.wait_ge(misc_free, 3)
            pe.wait_ge(first_apart, 1)
            pe.wait_ge(last_apart, 1)
            for i in range(8):
                maxima(0, 0, i)
            turn_maxima(0, 4)
            pe.wait_ge(misc_free, 5)
            pe.wait_ge(first_apart, 2)
            pe.wait_ge(last_apart, 2)
            for i in range(2):
                maxima(1, 1, i)
            project_values(5)
            with pe.Fori(0, B) as b:
                misc0 = b * MISC_SEQ + MISC_EARLY
                for g in range(GROUPS):
                    n = b * GROUPS + g
                    misc = misc0 + g * MISC_GROUP
                    pe.wait_ge(misc_free, misc if g == 0 else misc + 1)
                    for i in range(TILES * PER):
                        kb, j = i // PER, i % PER
                        pe.wait_ge(score_free, n * (TILES * PER) + i + 1)
                        out = score_ps[i % 2][:, 0:S - kb * P]
                        score(out, k_apart[g][:, j, kb * P:(kb + 1) * P], qm_rows[g % 2][:, kb * P:], 1, out[:, 0:P]).then_inc(score_full, 1)
                        if j == 1 and kb:
                            if kb == 1:
                                pe.wait_ge(divided, n + 1)
                                if g == 0:
                                    pe.wait_ge(result_full, b + 1)
                                    pe.wait_ge(misc_free, misc + 1)
                            multiply(g, n, kb - 1)
                        if i % 2 and i < 12:
                            maxima((g + 1) % GROUPS, n + 1, 2 + i // 2)
                        if i == 3:
                            if g == 2:
                                pe.wait_ge(seq_in, (b + 2) * 32)
                            project(wk, 1, (g + 2) % GROUPS, misc)
                        if i == 7:
                            project(wq, 0, (g + 2) % GROUPS, misc + 1)
                    pe.wait_ge(misc_free, misc + 3)
                    pe.wait_ge(first_apart, n + 3)
                    pe.wait_ge(last_apart, n + 3)
                    maxima((g + 2) % GROUPS, n + 2, 0)
                    maxima((g + 2) % GROUPS, n + 2, 1)
                    multiply(g, n, TILES - 1)
                    turn_maxima(n + 1, misc + 2)
                    pe.wait_ge(sums_moved, n + 1)
                    for i in range(TILES):
                        last = pe.transpose(sums_ps[:, i * P:(i + 1) * P], sums_t[:, i * P:(i + 1) * P], ident)
                    last.then_inc(sums_turned, 1)
                pe.wait_ge(divided, (b + 1) * GROUPS + 1)
                for i in range(TILES):
                    last = pe.transpose(sums_ps[:, i * P:(i + 1) * P], heads_out[:, i, :], ident)
                last.then_inc(heads_turned, 1)
                project_values(misc0 + GROUPS * MISC_GROUP)
                pe.wait_ge(heads_moved, b + 1)
                for i in range(TILES):
                    at = slice(i * P, (i + 1) * P)
                    last = pe.matmul(sums_ps[:, at], heads_out_t[:, at], wo[:, :], start=True, stop=True)
                last.then_inc(projected, 1)


def constants():
    c = np.zeros((P, C_END), np.float32)
    p = np.arange(P)
    c[:, C_IDENT:C_IDENT + P] = np.eye(P)
    c[E:2 * E, C_NEG_W] = -1
    row = p % 32
    c[(row >= 20) & (row < 28), C_NEG_Q] = -1
    c[(row >= 12) & (row < 20), C_NEG_K] = -1
    c[1, C_NEG_AUX] = -1
    c[:, C_RANK:C_RANK + TILES * N_GROUP] = 2 - np.tile(np.arange(N_GROUP), TILES)
    c[:, C_POW:C_POW + TILES] = -0.5
    c[:, C_MASK_Q:C_MASK_Q + P] = np.where(p[None, :] > p[:, None], -1e30, 0)
    c[:, C_MASK_K:C_MASK_K + P] = np.where(p[:, None] > p[None, :], -1e30, 0)
    c[0:2, C_AUX:] = 1
    c[2, C_AUX:] = np.arange(S)
    return c


def attention_constants():
    start = 2 ** (-2 ** (-(np.log2(HEADS) - 3)))
    slopes = np.array([start * start ** i for i in range(HEADS)], np.float32)
    bits = slopes.view(np.uint32)
    high = ((bits + 0x7ff + ((bits >> 12) & 1)) & np.uint32(0xfffff000)).view(np.float32)
    low = slopes - high
    c = np.zeros((3, 2, HEADS, 32), np.float32)
    q, k = c[:, 0], c[:, 1]
    q[0:2, :, 0], q[0:2, :, 2] = high, low
    k[0:2, :, 1], k[0:2, :, 3] = -high, -low
    q[2, :, [1, 3]] = 1
    k[2, :, [0, 2]] = 1
    k[0:2, :, 28:30] = 1
    return c.reshape(3, 2, HEADS * 32)


def program(nc, dram, phases=2):
    with ExitStack() as ctx:
        def sb(name, shape, dt=F32):
            return ctx.enter_context(nc.sbuf_tensor(name, shape, dt))

        t = {
            "x_rows": sb("x_rows", [P, (B + 2) * TILES, D]),
            "xt_hi": sb("xt_hi", [P, (B + 1) * S], F32R),
            "xt_lo": sb("xt_lo", [P, (B + 1) * S], F32R),
            "const": sb("const", [P, C_END]),
        }
        expert_phase(nc, t, dram)
        if phases == 2:
            attention_phase(nc, t, dram)
        else:
            with ExitStack() as c2:
                done = c2.enter_context(nc.semaphore("done"))
                block = c2.enter_context(nc.Block())
                @block.sync
                def _(sp):
                    sp.dma_start(dram["out"], t["x_rows"][:, TILES:(B + 1) * TILES, :]).then_inc(done, 16)
                    sp.wait_ge(done, 16)


def layout(a):
    f = {k: np.asarray(v) for k, v in a.items()}
    pair = lambda w, shared: np.concatenate([shared.T, w.transpose(2, 0, 1).reshape(D, E * I)], axis=1)
    down = f["L0_ffn_expert_down"].transpose(0, 2, 1).reshape(PAIRS, P, D).transpose(1, 0, 2)
    pick = np.zeros((2 * E, PAIRS, P), np.float32)
    for e in range(E):
        pick[[e, E + e], e // 2, (e % 2) * I:(e % 2 + 1) * I] = 1

    def padded(w, starts):
        out = np.zeros((w.shape[0], HEADS, 32), np.float32)
        for at in starts:
            out[:, :, at:at + DH] = w.reshape(-1, HEADS, DH)
        return out.reshape(-1, HEADS * 32)

    aux_bias = np.zeros((3, 2, HEADS * 32), np.float32)
    aux_bias[0:2, 0] = padded(f["L0_attn_bq"].reshape(1, D), (4, 12, 20))
    aux_bias[0:2, 1] = padded(f["L0_attn_bk"].reshape(1, D), (4, 12, 20))
    return {
        "x": f["L0_attn_x"].reshape(B * S, D),
        "const": constants(),
        "gate_w": f["L0_ffn_gate_w"].T,
        "gate_b": np.broadcast_to(f["L0_ffn_gate_bias"], (P, TILES, E)),
        "bo": f["L0_attn_bo"].reshape(D, 1),
        "pick": pick.reshape(2 * E, PAIRS * P),
        "wq": padded(f["L0_attn_Wq"].T, (4, 12, 20)),
        "wk": padded(f["L0_attn_Wk"].T, (4, 12, 20)),
        "wv": f["L0_attn_Wv"].T,
        "wo": f["L0_attn_Wo"].T,
        "bv": f["L0_attn_bv"].reshape(1, D),
        "aux_bias": aux_bias,
        "aux_const": attention_constants(),
        "wg": pair(f["L0_ffn_expert_gate"], f["L0_ffn_shared_gate"]),
        "wu": pair(f["L0_ffn_expert_up"], f["L0_ffn_shared_up"]),
        "wd": np.concatenate([f["L0_ffn_shared_down"].T[:, None, :], down], axis=1),
    }


def build(nc, arrays, phases=2):
    dram = {n: nc.dram_tensor("in_" + n, a.shape, mybir.dt.from_np(a.dtype), kind="ExternalInput").ap() for n, a in arrays.items()}
    dram["x"] = dram["x"].rearrange("(n p) d -> p n d", p=P)
    dram["out"] = nc.dram_tensor("out", (B, S, D), F32, kind="ExternalOutput").ap().rearrange("b (n p) d -> p (b n) d", p=P)
    program(nc, dram, phases)


def kernel(**inputs):
    import concourse.bacc as bacc
    from concourse.bass_utils import run_bass_kernel_spmd

    nc = bacc.Bacc("TRN2", target_bir_lowering=False, num_devices=1)
    arrays = {n: np.ascontiguousarray(a) for n, a in layout(inputs).items()}
    build(nc, arrays)
    r = run_bass_kernel_spmd(nc, [{"in_" + n: a for n, a in arrays.items()}], core_ids=[0])
    return r.results[0]["out"]
```

```python
from contextlib import ExitStack

import numpy as np

import concourse.bass as bass
from concourse import mybir

F32 = mybir.dt.float32
F32R = mybir.dt.float32r
ALU = mybir.AluOpType
ACT = mybir.ActivationFunctionType
AX = mybir.AxisListType

P = 128
B, S, D = 16, 512, 128
TILES = S // P
HEADS, DH = 16, 8
PER, GROUPS = 4, 4
E, I = 32, 64
N_GROUP, TOP_K = 4, 8
PER_GROUP = E // N_GROUP
ROUTED_SCALING = 2.5
EPS = 1e-5
PAIRS = E // 2
UNITS = PAIRS + 1
NEVER = -3e38
WARM = 30
PREP_INPUTS, PREP_LOGITS, PREP_WEIGHTS = 5, 6, 16
FINISH = 3

C_IDENT = 0
C_NEG_W = C_IDENT + P
C_NEG_Q = C_NEG_W + 1
C_NEG_K = C_NEG_Q + 1
C_NEG_AUX = C_NEG_K + 1
C_RANK = C_NEG_AUX + 1
C_POW = C_RANK + TILES * N_GROUP
C_MASK_Q = C_POW + TILES
C_MASK_K = C_MASK_Q + P
C_AUX = C_MASK_K + P
C_END = C_AUX + S


def rows_of(x_rows, b):
    return x_rows[:, bass.ds((b + 1) * TILES, TILES), :]


def expert_phase(nc, t, dram):
    with ExitStack() as ctx:
        def sb(name, shape, dt=F32):
            return ctx.enter_context(nc.sbuf_tensor(name, shape, dt))

        def psum(name, shape):
            return ctx.enter_context(nc.psum_tensor(name, shape, F32))

        def sem(name):
            return ctx.enter_context(nc.semaphore(name))

        x_rows, xt_hi, xt_lo, const = t["x_rows"], t["xt_hi"], t["xt_lo"], t["const"]
        ident = const[:, C_IDENT:C_IDENT + P]
        WIDE = PAIRS * P
        later = x_rows[:, 4 * TILES:(B + 2) * TILES, :].rearrange("p n d -> p (n d)")
        wg_raw, wu_raw, wd_raw = [later[:, n * (WIDE + P):(n + 1) * (WIDE + P)] for n in range(3)]
        wg_hi, wg_lo = sb("wg_hi", [P, WIDE + P], F32R), sb("wg_lo", [P, WIDE + P], F32R)
        wu_hi, wu_lo = sb("wu_hi", [P, WIDE + P], F32R), sb("wu_lo", [P, WIDE + P], F32R)
        wd_hi, wd_lo = sb("wd_hi", [P, WIDE + P], F32R), sb("wd_lo", [P, WIDE + P], F32R)
        gate_w = sb("gate_w", [P, E])
        gate_b = sb("gate_b", [P, TILES, E])
        bo = sb("bo", [P, 1])
        pick = sb("pick", [2 * E, PAIRS, P], F32R)

        stats = sb("stats", [P, TILES, 6])
        mean_var = sb("mean_var", [P, TILES, 2])
        var_eps = sb("var_eps", [P, TILES])
        rstd = sb("rstd", [P, TILES])
        xn = sb("xn", [P, TILES, D])
        xt_raw = sb("xt_raw", [P, S])
        th = sb("th", [P, TILES, E])
        scores = sb("scores", [P, TILES, E])
        choice = sb("choice", [P, TILES, E])
        TG = TILES * N_GROUP
        hi1, lo1 = sb("hi1", [P, TG, 4]), sb("lo1", [P, TG, 4])
        hi2, lo2a = sb("hi2", [P, TG, 2]), sb("lo2a", [P, TG, 2])
        lo2b, lo2 = sb("lo2b", [P, TG, 2]), sb("lo2", [P, TG, 2])
        hi3, lo3a = sb("hi3", [P, TG]), sb("lo3a", [P, TG])
        lo3b, lo3 = sb("lo3b", [P, TG]), sb("lo3", [P, TG])
        group_score = sb("group_score", [P, TILES, N_GROUP])
        beats = [sb(f"beats{d}", [P, TILES, N_GROUP + d]) for d in (1, 2, 3)]
        net = [sb(f"net{d}", [P, TILES, N_GROUP]) for d in (1, 2, 3)]
        group_on = sb("group_on", [P, TILES, N_GROUP])
        masked = sb("masked", [P, TILES, E])
        top8 = sb("top8", [P, TILES, TOP_K])
        taken = sb("taken", [P, TILES, E])
        chosen = sb("chosen", [P, TILES, E])
        w_sum = sb("w_sum", [P, TILES])
        spare = sb("spare", [P, 1])
        w_row = sb("w_row", [P, TILES, 2, E])
        wt_round = sb("wt_round", [2 * E, S], F32R)
        wt = sb("wt", [2 * E, S], F32R)

        silu = [sb(f"silu{n}", [P, S]) for n in range(2)]
        hidden = [sb("hidden%d" % i, [P, S]) for i in range(2)]
        weighted = [sb(f"weighted{n}", [P, S]) for n in range(2)]
        w_hi = [sb(f"w_hi{n}", [P, S], F32R) for n in range(2)]
        w_lo = [sb(f"w_lo{n}", [P, S], F32R) for n in range(2)]
        pick_raw = silu + hidden
        ffn_t = sb("ffn_t", [D, S])

        gate_ps = [psum(f"gate_ps{n}", [P, S]) for n in range(2)]
        up_ps = [psum(f"up_ps{n}", [P, S]) for n in range(2)]
        spread_ps = [psum(f"spread_ps{n}", [P, S]) for n in range(2)]
        ffn_ps = psum("ffn_ps", [P, S])
        prep_ps = psum("prep_ps", [P, S])

        x_in = [sem("x_in0"), sem("x_in1")]
        const_in = sem("const_in")
        small_in = sem("small_in")
        pick_in = sem("pick_in")
        wg_in, wu_in, wd_in = sem("wg_in"), sem("wu_in"), sem("wd_in")
        zeroed = sem("zeroed")
        w_rounded = sem("w_rounded")
        w_split = sem("w_split")
        wd_split = sem("wd_split")
        picked = sem("picked")
        has_var, has_rstd, has_xn = sem("has_var"), sem("has_rstd"), sem("has_xn")
        has_xt = sem("has_xt")
        has_w_row = sem("has_w_row")
        has_wt_round = sem("has_wt_round")
        step = sem("step")
        prep_full, prep_free = sem("prep_full"), sem("prep_free")
        gate_full, gate_free = sem("gate_full"), sem("gate_free")
        up_full, up_free = sem("up_full"), sem("up_free")
        spread_full, spread_free = sem("spread_full"), sem("spread_free")
        ffn_free = sem("ffn_free")
        hi_full, hi_used = sem("hi_full"), sem("hi_used")
        lo_full, lo_used = sem("lo_full"), sem("lo_used")

        PREP_USES, PREP_EARLY = 4, 3

        block = ctx.enter_context(nc.Block())

        @block.sync
        def _(sp):
            sp.dma_start(rows_of(x_rows, 0), dram["x"][:, 0:TILES, :]).then_inc(x_in[0], 16)
            sp.dma_start(const[:, :], dram["const"]).then_inc(const_in, 16)
            sp.dma_start(gate_w[:, :], dram["gate_w"]).then_inc(small_in, 16)
            sp.dma_start(gate_b[:, :, :], dram["gate_b"]).then_inc(small_in, 16)
            sp.dma_start(bo[:, :], dram["bo"]).then_inc(small_in, 16)
            sp.dma_start(wg_raw, dram["wg"]).then_inc(wg_in, 16)
            sp.dma_start(wu_raw, dram["wu"]).then_inc(wu_in, 16)
            sp.dma_start(wd_raw, dram["wd"]).then_inc(wd_in, 16)
            sp.dma_start(rows_of(x_rows, 1), dram["x"][:, TILES:2 * TILES, :]).then_inc(x_in[1], 16)
            for n in range(4):
                sp.dma_start(pick_raw[n][0:2 * E, :], dram["pick"][:, n * S:(n + 1) * S]).then_inc(pick_in, 16)
            sp.wait_ge(w_split, 2)
            sp.wait_ge(wd_split, 1)
            with sp.Fori(1, B // 2) as it:
                for half in range(2):
                    sp.wait_ge(x_in[half], it * 16)
                    b = it * 2 + half
                    sp.dma_start(rows_of(x_rows, b), dram["x"][:, bass.ds(b * TILES, TILES), :]).then_inc(x_in[half], 16)
            sp.wait_ge(x_in[0], B // 2 * 16)
            sp.dma_start(rows_of(x_rows, B), dram["x"][:, 0:TILES, :]).then_inc(x_in[0], 16)

        @block.gpsimd
        def _(pool):
            for d in range(3):
                pool.memset(beats[d][:, :, :], 0.0).then_inc(zeroed, 1)
            for n in range(2):
                pool.memset(weighted[n][:, :], 0.0).then_inc(zeroed, 1)
                pool.memset(w_hi[n][:, :].bitcast(F32), 0.0).then_inc(zeroed, 1)
                pool.memset(w_lo[n][:, :].bitcast(F32), 0.0).then_inc(zeroed, 1)
            pool.memset(x_rows[:, 0:TILES, :], 0.0).then_inc(zeroed, 1)
            pool.wait_ge(const_in, 16)

            def inverse_deviation(count):
                pool.wait_ge(has_var, count)
                pool.tensor_tensor(rstd[:, :], var_eps[:, :], const[:, C_POW:C_POW + TILES], ALU.pow).then_inc(has_rstd, 1)

            inverse_deviation(1)
            pool.wait_ge(w_rounded, 2)
            pool.tensor_tensor(wu_lo[:, :], wu_raw, wu_hi[:, :].bitcast(F32), ALU.subtract).then_inc(w_split, 1)
            pool.wait_ge(w_rounded, 3)
            pool.tensor_tensor(wd_lo[:, :], wd_raw, wd_hi[:, :].bitcast(F32), ALU.subtract).then_inc(wd_split, 1)
            with pool.Fori(0, B // 2) as it:
                for half in range(2):
                    for u in range(UNITS):
                        k = half * UNITS + u
                        done = it * (2 * UNITS) + k
                        pool.wait_ge(hi_full, done + 3)
                        pool.wait_ge(lo_used, done + 2)
                        pool.tensor_tensor(w_lo[k % 2][:, :], weighted[k % 2][:, :], w_hi[k % 2][:, :].bitcast(F32), ALU.subtract).then_inc(lo_full, 1)
                        if u == 0:
                            inverse_deviation(it * 2 + half + 2)

        @block.scalar
        def _(act):
            act.sem_inc(gate_free, 2)
            act.sem_inc(hi_full, 1)
            act.sem_inc(hi_used, 1)
            act.sem_inc(lo_full, 3)

            def copy_inputs(n, splits):
                if splits is not None:
                    act.wait_ge(has_xt, splits)
                act.wait_ge(prep_full, n)
                act.copy(xt_raw[:, :], prep_ps[:, :]).then_inc(prep_free, 1)

            def gate_tanh(n):
                act.wait_ge(prep_full, n)
                act.activation(th[:, :, :].rearrange("p t e -> p (t e)"), prep_ps[:, 0:TILES * E], ACT.Tanh, scale=0.5).then_inc(prep_free, 1)

            def round_weights(n):
                act.wait_ge(prep_full, n)
                act.copy(wt_round[:, :], prep_ps[0:2 * E, :]).then_inc(has_wt_round, 1)

            copy_inputs(1, None)
            gate_tanh(2)
            act.wait_ge(wg_in, 16)
            act.copy(wg_hi[:, :], wg_raw).then_inc(w_rounded, 1)
            act.wait_ge(wu_in, 16)
            act.copy(wu_hi[:, :], wu_raw).then_inc(w_rounded, 1)
            act.wait_ge(small_in, 48)
            act.wait_ge(pick_in, 64)
            for n in range(4):
                act.copy(pick[:, 4 * n:4 * n + 4, :].rearrange("p a b -> p (a b)"), pick_raw[n][0:2 * E, :]).then_inc(picked, 1)
            act.wait_ge(wd_in, 16)
            act.copy(wd_hi[:, :], wd_raw).then_inc(w_rounded, 1)
            round_weights(3)
            act.wait_ge(picked, 4)

            def round_weighted(done, b, u, slot):
                if u == 1:
                    act.wait_ge(up_free, done + 2)
                elif u == 0:
                    act.wait_ge(spread_free, b * PAIRS + 2)
                else:
                    act.wait_ge(spread_free, b * PAIRS + u + 1)
                act.wait_ge(hi_used, done + 1)
                act.wait_ge(lo_full, done + 1)
                act.copy(w_hi[slot][:, :], weighted[slot][:, :]).then_inc(hi_full, 1)

            def finish_ffn(b):
                act.wait_ge(lo_used, (b + 1) * UNITS + 3)
                act.wait_ge(prep_free, (b + 1) * PREP_USES + 1)
                act.activation(ffn_t[:, :], ffn_ps[:, :], ACT.Identity, bias=bo[:, 0:1]).then_inc(ffn_free, 1)

            with act.Fori(0, B // 2) as it:
                for half in range(2):
                    b = it * 2 + half
                    uses = b * PREP_USES + PREP_EARLY
                    for u in range(UNITS):
                        k = half * UNITS + u
                        done = it * (2 * UNITS) + k
                        if u == 2:
                            finish_ffn(b - 1)
                        act.wait_ge(gate_full, done + 1)
                        act.wait_ge(up_free, done + 1)
                        act.activation(silu[k % 2][:, :], gate_ps[k % 2][:, :], ACT.Silu).then_inc(gate_free, 1)
                        round_weighted(done, b, u, (k + 1) % 2)
                        if u == PREP_INPUTS:
                            copy_inputs(uses + 2, b + 1)
                        if u == PREP_LOGITS:
                            gate_tanh(uses + 3)
                        if u == PREP_WEIGHTS:
                            round_weights(uses + 4)
            round_weighted(B * UNITS, B, 0, (B * UNITS + 1) % 2)
            finish_ffn(B - 1)

        @block.vector
        def _(dve):
            V = nc.vector
            dve.sem_inc(prep_free, 1)
            dve.sem_inc(up_free, 2)
            dve.sem_inc(spread_free, 2)
            count = [0, 0]

            def then(instruction):
                instruction.then_inc(step, 1)
                count[1] += 1
                dve.wait_ge(step, count[0] + count[1])

            def variance(b):
                rows = rows_of(x_rows, b)
                for i in range(TILES):
                    last = V.bn_stats(stats[:, i, :], rows[:, i, :])
                then(last)
                V.memset(spare[:, :], 0.0)
                for i in range(TILES):
                    last = V.bn_aggr(mean_var[:, i, :], stats[:, i, :])
                then(last)
                V.tensor_scalar(var_eps[:, :], mean_var[:, :, 1], EPS, None, ALU.add).then_inc(has_var, 1)

            def normalise(b, n):
                rows = rows_of(x_rows, b)
                dve.wait_ge(has_rstd, n)
                for i in range(TILES):
                    last = V.tensor_scalar(xn[:, i, :], rows[:, i, :], mean_var[:, i, 0:1], rstd[:, i:i + 1], ALU.subtract, ALU.mult)
                last.then_inc(has_xn, 1)

            def split_inputs(b, n):
                dve.wait_ge(prep_free, n)
                at = bass.ds(b * S, S)
                then(V.tensor_copy(xt_hi[:, at], xt_raw[:, :]))
                V.tensor_tensor(xt_lo[:, at], xt_raw[:, :], xt_hi[:, at].bitcast(F32), ALU.subtract).then_inc(has_xt, 1)

            def grp(a):
                return a[:, :, :].rearrange("p t (g e) -> p (t g) e", g=N_GROUP)

            def score_experts(n):
                dve.wait_ge(prep_free, n)
                then(V.tensor_scalar(scores[:, :, :], th[:, :, :], 0.5, 0.5, ALU.mult, ALU.add))
                then(V.tensor_tensor(choice[:, :, :], scores[:, :, :], gate_b[:, :, :], ALU.add))

            def pair_off():
                c = grp(choice)
                V.tensor_tensor(hi1[:, :, :], c[:, :, 0:4], c[:, :, 4:8], ALU.max)
                then(V.tensor_tensor(lo1[:, :, :], c[:, :, 0:4], c[:, :, 4:8], ALU.min))
                V.tensor_tensor(hi2[:, :, :], hi1[:, :, 0:2], hi1[:, :, 2:4], ALU.max)
                V.tensor_tensor(lo2a[:, :, :], hi1[:, :, 0:2], hi1[:, :, 2:4], ALU.min)
                then(V.tensor_tensor(lo2b[:, :, :], lo1[:, :, 0:2], lo1[:, :, 2:4], ALU.max))
                then(V.tensor_tensor(lo2[:, :, :], lo2a[:, :, :], lo2b[:, :, :], ALU.max))

            def group_scores():
                V.tensor_tensor(hi3[:, :], hi2[:, :, 0], hi2[:, :, 1], ALU.max)
                V.tensor_tensor(lo3a[:, :], hi2[:, :, 0], hi2[:, :, 1], ALU.min)
                then(V.tensor_tensor(lo3b[:, :], lo2[:, :, 0], lo2[:, :, 1], ALU.max))
                then(V.tensor_tensor(lo3[:, :], lo3a[:, :], lo3b[:, :], ALU.max))
                then(V.tensor_tensor(group_score[:, :, :].rearrange("p t g -> p (t g)"), hi3[:, :], lo3[:, :], ALU.add))

            def choose_groups():
                g = group_score
                for d in (1, 2, 3):
                    last = V.tensor_tensor(beats[d - 1][:, :, d:N_GROUP], g[:, :, 0:N_GROUP - d], g[:, :, d:N_GROUP], ALU.is_ge)
                then(last)
                for d in (1, 2, 3):
                    last = V.tensor_tensor(net[d - 1][:, :, :], beats[d - 1][:, :, d:N_GROUP + d], beats[d - 1][:, :, 0:N_GROUP], ALU.subtract)
                then(last)
                then(V.tensor_tensor(net[0][:, :, :], net[0][:, :, :], net[1][:, :, :], ALU.add))
                then(V.tensor_tensor(net[0][:, :, :], net[0][:, :, :], net[2][:, :, :], ALU.add))

            def mask_groups():
                rank = const[:, C_RANK:C_RANK + TG].rearrange("p (t g) -> p t g", t=TILES)
                then(V.tensor_tensor(group_on[:, :, :], net[0][:, :, :], rank, ALU.is_ge))
                on = group_on[:, :, :].rearrange("p t g -> p (t g)").unsqueeze(2).to_broadcast([P, TG, PER_GROUP])
                then(V.tensor_tensor(grp(masked), grp(choice), on, ALU.mult))
                then(V.tensor_scalar(masked[:, :, :], masked[:, :, :], 0.0, None, ALU.add))

            def choose_experts():
                for i in range(TILES):
                    last = V.max(top8[:, i, :], masked[:, i, :])
                then(last)

            def mark_experts():
                V.memset(spare[:, :], 0.0)
                for i in range(TILES):
                    last = V.match_replace(taken[:, i, :], top8[:, i, :], masked[:, i, :], NEVER)
                then(last)
                then(V.tensor_tensor(chosen[:, :, :], taken[:, :, :], masked[:, :, :], ALU.not_equal))
                then(V.tensor_tensor(chosen[:, :, :], chosen[:, :, :], scores[:, :, :], ALU.mult))

            def weigh_experts():
                then(V.tensor_reduce(w_sum[:, :], chosen[:, :, :], AX.X, ALU.add))
                then(V.tensor_scalar(w_sum[:, :], w_sum[:, :], 1e-20, None, ALU.add))
                then(V.reciprocal(w_sum[:, :], w_sum[:, :]))
                then(V.tensor_scalar(w_sum[:, :], w_sum[:, :], ROUTED_SCALING, None, ALU.mult))
                over = w_sum[:, :].unsqueeze(2).to_broadcast([P, TILES, E])
                for n in range(2):
                    last = V.tensor_tensor(w_row[:, :, n, :], chosen[:, :, :], over, ALU.mult)
                last.then_inc(has_w_row, 1)

            def split_weights(n):
                dve.wait_ge(has_wt_round, n)
                V.scalar_tensor_tensor(wt[:, :], wt_round[:, :].bitcast(F32), const[0:2 * E, C_NEG_W:C_NEG_W + 1],
                                       prep_ps[0:2 * E, :], ALU.mult, ALU.add).then_inc(prep_free, 1)

            def add_output(b):
                dve.wait_ge(prep_full, (b + 1) * PREP_USES + PREP_EARLY + 1)
                rows = rows_of(x_rows, b)
                V.tensor_tensor(rows, prep_ps[:, :].rearrange("p (t d) -> p t d", t=TILES), rows, ALU.add).then_inc(prep_free, 1)

            dve.wait_ge(const_in, 16)
            dve.wait_ge(zeroed, 10)
            dve.wait_ge(x_in[0], 16)
            variance(0)
            normalise(0, 1)
            split_inputs(0, 2)
            dve.wait_ge(small_in, 48)
            score_experts(3)
            for route in (pair_off, group_scores, choose_groups, mask_groups, choose_experts, mark_experts, weigh_experts):
                route()
            steps_each = count[1]
            dve.wait_ge(w_rounded, 1)
            V.tensor_tensor(wg_lo[:, :], wg_raw, wg_hi[:, :].bitcast(F32), ALU.subtract).then_inc(w_split, 1)
            split_weights(1)
            with dve.Fori(0, B // 2) as it:
                for half in range(2):
                    b = it * 2 + half
                    uses = b * PREP_USES + PREP_EARLY
                    count[0] = (b + 1) * steps_each
                    count[1] = 0
                    for u in range(UNITS):
                        k = half * UNITS + u
                        done = it * (2 * UNITS) + k
                        dve.wait_ge(up_full, done + 1)
                        dve.wait_ge(gate_free, done + 3)
                        if u == 0:
                            dve.wait_ge(lo_full, done + 2)
                            V.tensor_tensor(weighted[k % 2][:, :], up_ps[k % 2][:, :], silu[k % 2][:, :], ALU.mult).then_inc(up_free, 1)
                        else:
                            V.tensor_tensor(hidden[k % 2][:, :], up_ps[k % 2][:, :], silu[k % 2][:, :], ALU.mult).then_inc(up_free, 1)
                            pair = b * PAIRS + u - 1
                            dve.wait_ge(up_free, done + 3)
                            dve.wait_ge(spread_full, pair + 1)
                            dve.wait_ge(lo_full, done + 2)
                            V.tensor_tensor(weighted[k % 2][:, :], spread_ps[(u - 1) % 2][:, :], hidden[k % 2][:, :], ALU.mult).then_inc(spread_free, 1)
                        if u == FINISH:
                            add_output(b - 1)
                        if u == 1:
                            dve.wait_ge(x_in[1 - half], (it + 1 + half) * 16)
                            variance(b + 1)
                        if u == 2:
                            normalise(b + 1, b + 2)
                        if u == PREP_INPUTS + 1:
                            split_inputs(b + 1, uses + 3)
                        if u == PREP_LOGITS + 1:
                            score_experts(uses + 4)
                        if u == PREP_LOGITS + 2:
                            pair_off()
                        if u == PREP_LOGITS + 3:
                            group_scores()
                        if u == PREP_LOGITS + 4:
                            choose_groups()
                        if u == PREP_LOGITS + 5:
                            mask_groups()
                        if u == PREP_LOGITS + 6:
                            choose_experts()
                        if u == PREP_LOGITS + 7:
                            mark_experts()
                        if u == PREP_LOGITS + 8:
                            weigh_experts()
                    split_weights(b + 2)
            add_output(B - 1)
            assert count[1] == steps_each

        @block.tensor
        def _(pe):
            def transpose_inputs(n, use):
                pe.wait_ge(has_xn, n)
                pe.wait_ge(prep_free, use + 1)
                for i in range(TILES):
                    last = pe.transpose(prep_ps[:, i * P:(i + 1) * P], xn[:, i, :], ident)
                last.then_inc(prep_full, 1)

            def route(use):
                pe.wait_ge(prep_free, use + 1)
                for i in range(TILES):
                    last = pe.matmul(prep_ps[:, i * E:(i + 1) * E], xt_raw[:, i * P:(i + 1) * P], gate_w[:, :], start=True, stop=True)
                last.then_inc(prep_full, 1)

            def transpose_weights(n, use):
                pe.wait_ge(has_w_row, n)
                pe.wait_ge(prep_free, use + 1)
                for i in range(TILES):
                    last = pe.matmul(prep_ps[0:2 * E, i * P:(i + 1) * P], w_row[:, i, :, :].rearrange("p a e -> p (a e)"), ident, start=True, stop=True)
                last.then_inc(prep_full, 1)

            def transpose_output(b):
                pe.wait_ge(ffn_free, b + 2)
                pe.wait_ge(prep_free, (b + 1) * PREP_USES + PREP_EARLY + 1)
                for i in range(TILES):
                    last = pe.transpose(prep_ps[:, i * P:(i + 1) * P], ffn_t[:, i * P:(i + 1) * P], ident)
                last.then_inc(prep_full, 1)

            def project(out, hi, lo, u, x_hi, x_lo):
                at = slice(u * P, (u + 1) * P)
                pe.matmul(out[:, :], hi[:, at], x_hi, start=True, stop=False)
                pe.matmul(out[:, :], hi[:, at], x_lo, start=False, stop=False)
                return pe.matmul(out[:, :], lo[:, at], x_hi, start=False, stop=True)

            def down_hi(done, b, u, slot):
                if u == 0:
                    pe.wait_ge(ffn_free, b + 1)
                if u == UNITS - 2:
                    pe.wait_ge(wd_split, 1)
                pe.wait_ge(hi_full, done + 1)
                at = slice(u * P, (u + 1) * P)
                pe.matmul(ffn_ps[:, :], wd_hi[:, at], w_hi[slot][:, :], start=u == 0, stop=False)
                pe.matmul(ffn_ps[:, :], wd_lo[:, at], w_hi[slot][:, :], start=False, stop=False).then_inc(hi_used, 1)

            def down_lo(done, u, slot):
                pe.wait_ge(lo_full, done + 1)
                pe.matmul(ffn_ps[:, :], wd_hi[:, u * P:(u + 1) * P], w_lo[slot][:, :], start=False, stop=u == UNITS - 1).then_inc(lo_used, 1)

            pe.wait_ge(const_in, 16)
            transpose_inputs(1, 0)
            pe.wait_ge(small_in, 48)
            route(1)
            transpose_weights(1, 2)
            pe.wait_ge(w_split, 2)
            pe.wait_ge(picked, 4)
            pe.wait_ge(zeroed, 10)
            pe.wait_ge(w_rounded, 3)
            pe.matmul(ffn_ps[:, :], wd_hi[:, 0:P], w_hi[0][:, :], start=True, stop=False)
            with pe.Fori(0, B // 2) as it:
                for half in range(2):
                    b = it * 2 + half
                    uses = b * PREP_USES + PREP_EARLY
                    x_hi, x_lo = xt_hi[:, bass.ds(b * S, S)], xt_lo[:, bass.ds(b * S, S)]
                    pe.wait_ge(has_xt, b + 1)
                    for u in range(UNITS):
                        k = half * UNITS + u
                        done = it * (2 * UNITS) + k
                        pe.wait_ge(gate_free, done + 1)
                        project(gate_ps[k % 2], wg_hi, wg_lo, u, x_hi, x_lo).then_inc(gate_full, 1)
                        down_lo(done, (u - 3) % UNITS, (k + 1) % 2)
                        if u == FINISH:
                            transpose_output(b - 1)
                        pe.wait_ge(up_free, done + 1)
                        project(up_ps[k % 2], wu_hi, wu_lo, u, x_hi, x_lo).then_inc(up_full, 1)
                        if u:
                            pair = b * PAIRS + u - 1
                            if u == 1:
                                pe.wait_ge(prep_free, uses + 1)
                            pe.wait_ge(spread_free, pair + 1)
                            pe.matmul(spread_ps[(u - 1) % 2][:, :], pick[:, u - 1, :], wt[:, :], start=True, stop=True).then_inc(spread_full, 1)
                        down_hi(done, b, (u - 2) % UNITS, k % 2)
                        if u == PREP_INPUTS:
                            transpose_inputs(b + 2, uses + 1)
                        if u == PREP_LOGITS:
                            route(uses + 2)
                        if u == PREP_WEIGHTS:
                            transpose_weights(b + 2, uses + 3)
            for n in range(3):
                down_lo(B * UNITS + n, UNITS - 3 + n, (n + 1) % 2)
                if n < 2:
                    down_hi(B * UNITS + n, B - 1, UNITS - 2 + n, n)
            transpose_output(B - 1)


def attention_phase(nc, t, dram):
    with ExitStack() as ctx:
        def sb(name, shape, dt=F32):
            return ctx.enter_context(nc.sbuf_tensor(name, shape, dt))

        def psum(name, shape):
            return ctx.enter_context(nc.psum_tensor(name, shape, F32))

        def sem(name):
            return ctx.enter_context(nc.semaphore(name))

        x_rows, xt_hi, xt_lo, const = t["x_rows"], t["xt_hi"], t["xt_lo"], t["const"]
        ident = const[:, C_IDENT:C_IDENT + P]
        GW = GROUPS * P

        weights = sb("weights", [P, 2 * PER, S])
        wq_raw, wk_raw, wv_raw = weights[:, 0, :], weights[:, 1, :], weights[:, 2, 0:D]
        aux_raw, aux_const = weights[0:3, 4:6, :], weights[0:3, 6:8, :]
        wq = [sb("wq_hi", [D, GW], F32R), sb("wq_lo", [D, GW], F32R)]
        wk = [sb("wk_hi", [D, GW], F32R), sb("wk_lo", [D, GW], F32R)]
        aux = sb("aux", [3, 2, GW], F32R)
        aux_rows = sb("aux_rows", [3, S], F32R)
        masks = sb("masks", [P, 2, P], F32R)
        ident_r = sb("ident_r", [P, P], F32R)
        wv = [sb("wv_hi", [D, D], F32R), sb("wv_lo", [D, D], F32R)]
        wo, bv = sb("wo", [D, D]), sb("bv", [P, D])

        x_seq = [sb("x_seq_hi", [D, S], F32R), sb("x_seq_lo", [D, S], F32R)]
        rounded = sb("rounded", [P, S], F32R)
        q_rows = [sb(f"q_rows{g}", [P, S], F32R) for g in range(2)]
        qm_rows = [sb(f"qm_rows{g}", [P, S], F32R) for g in range(2)]
        k_rows = [sb(f"k_rows{g}", [P, S], F32R) for g in range(2)]
        k_apart = [sb(f"k_apart{g}", [P, PER, S], F32R) for g in range(GROUPS)]
        neg_max = [sb(f"neg_max{n}", [P, TILES, PER]) for n in range(2)]
        max_cols = sb("max_cols", [P, TILES, P], F32R)
        values = sb("values", [P, TILES, HEADS, 32])
        sums_t = sb("sums_t", [P, S])
        divisor = sb("divisor", [P, TILES, PER])
        heads_out = sb("heads_out", [P, TILES, D])
        heads_out_t = sums_t
        result = sb("result", [P, TILES, D])

        max_ps = [psum(f"max_ps{n}", [P, 2, S]) for n in range(2)]
        score_ps = [psum(f"score_ps{n}", [P, S]) for n in range(2)]
        sums_ps = psum("sums_ps", [P, S])
        misc_ps = psum("misc_ps", [P, S])

        weights_in = sem("weights_in")
        zeroed = sem("zeroed")
        weights_scaled, aux_summed, aux_rounded = sem("weights_scaled"), sem("aux_summed"), sem("aux_rounded")
        weights_rounded, weights_split = sem("weights_rounded"), sem("weights_split")
        ones_set = sem("ones_set")
        seq_in = sem("seq_in")
        misc_full, misc_free = sem("misc_full"), sem("misc_free")
        qk_rounded = sem("qk_rounded")
        first_apart, last_apart = sem("first_apart"), sem("last_apart")
        max_full, max_free = sem("max_full"), sem("max_free")
        max_high, max_split = sem("max_high"), sem("max_split")
        score_full, score_free = sem("score_full"), sem("score_free")
        weights_free = sem("weights_free")
        sums_moved, sums_turned, divided, has_divisor = sem("sums_moved"), sem("sums_turned"), sem("divided"), sem("has_divisor")
        heads_turned, heads_moved = sem("heads_turned"), sem("heads_moved")
        projected, result_full, result_out = sem("projected"), sem("result_full"), sem("result_out")

        MISC_EARLY, MISC_GROUP, MISC_SEQ = 6, 3, 3 * GROUPS + 1
        MAXIMA = [((3,), (0, 1)), ((3,), (2, 3)), ((2, 0), (0, 1)), ((2, 0), (2, 3)), ((1,), (0, 1, 2, 3))]
        SCORES = [((0,), (j,)) for j in range(PER)] + [((3, 1), (j,)) for j in range(PER)] + [((2,), (0, 1)), ((2,), (2, 3))]
        NM, NS = len(MAXIMA), len(SCORES)
        scored = [4, 8, 10, 8]

        block = ctx.enter_context(nc.Block())

        @block.sync
        def _(sp):
            for dst, name in ((aux_raw, "aux_bias"), (aux_const, "aux_const"), (wk_raw, "wk"), (wq_raw, "wq"), (wv_raw, "wv"),
                              (wo[:, :], "wo"), (bv[:, :], "bv")):
                sp.dma_start(dst, dram[name]).then_inc(weights_in, 16)

            def load_sequence(b):
                for dst, src in zip(x_seq, (xt_hi, xt_lo)):
                    sp.dma_start(dst[:, :].bitcast(F32), src[:, bass.ds(b * S, S)].bitcast(F32)).then_inc(seq_in, 16)

            load_sequence(0)
            with sp.Fori(0, B) as b:
                sp.wait_ge(misc_full, b * MISC_SEQ + MISC_EARLY + MISC_GROUP + 2)
                load_sequence(b + 1)
                sp.wait_ge(result_full, b + 2)
                sp.dma_start(dram["out"][:, bass.ds(b * TILES, TILES), :], result[:, :, :]).then_inc(result_out, 16)
            sp.wait_ge(result_out, (B + 2) * 16)
            sp.wait_ge(seq_in, (B + 1) * 32)

        @block.gpsimd
        def _(pool):
            pool.memset(max_cols[:, :, :].bitcast(F32), 0.0).then_inc(zeroed, 1)
            pool.memset(values[:, :, :, :], 0.0).then_inc(zeroed, 1)
            pool.memset(heads_out[:, :, :], 0.0).then_inc(zeroed, 1)
            pool.memset(sums_t[:, :], 1.0).then_inc(zeroed, 1)
            pool.wait_ge(zeroed, 4)
            pool.memset(values[:, :, :, DH:DH + 1], 1.0).then_inc(ones_set, 1)
            for g in range(GROUPS):
                pool.memset(k_apart[g][:, :, :].bitcast(F32), 0.0).then_inc(zeroed, 1)

        @block.scalar
        def _(act):
            act.sem_inc(score_free, 2)
            act.sem_inc(sums_moved, 1)
            act.wait_ge(weights_in, 7 * 16)
            act.copy(wk[0][:, :], wk_raw).then_inc(weights_rounded, 1)
            act.mul(wq_raw, wq_raw, DH ** -0.5).then_inc(weights_scaled, 1)
            act.wait_ge(aux_summed, 1)
            act.copy(aux[:, :, :], aux_const).then_inc(aux_rounded, 1)
            act.copy(aux_rows[:, :], const[0:3, C_AUX:C_AUX + S]).then_inc(ones_set, 1)
            act.wait_ge(weights_scaled, 1)
            act.copy(wq[0][:, :], wq_raw).then_inc(weights_rounded, 1)
            act.copy(ident_r[:, :], ident)
            act.copy(masks[:, :, :].rearrange("p a b -> p (a b)"), const[:, C_MASK_Q:C_MASK_Q + 2 * P])
            act.copy(wv[0][:, :], wv_raw).then_inc(weights_rounded, 1)

            def round_projection(misc):
                act.wait_ge(misc_full, misc + 1)
                act.copy(rounded[:, :], misc_ps[:, :]).then_inc(qk_rounded, 1)

            def set_apart(g, split):
                act.wait_ge(misc_free, split)
                rows = slice(32 * (PER - 1), 32 * PER)
                act.copy(k_apart[g][rows, PER - 1, :], k_rows[g % 2][rows, :].bitcast(F32)).then_inc(last_apart, 1)

            def move_heads(b):
                act.wait_ge(heads_turned, b + 1)
                act.copy(heads_out_t[:, :], sums_ps[:, :]).then_inc(heads_moved, 1)

            act.wait_ge(zeroed, 8)
            for n in range(4):
                round_projection(n)
                if n % 2:
                    set_apart(n // 2, n + 1)
            with act.Fori(0, B) as b:
                misc0 = b * MISC_SEQ + MISC_EARLY
                for g in range(GROUPS):
                    n = b * GROUPS + g
                    misc = misc0 + g * MISC_GROUP
                    for i, (tiles, heads) in enumerate(SCORES):
                        kb = tiles[-1]
                        cols = S // len(heads)
                        if i == 0:
                            act.wait_ge(weights_free, n * TILES + 2)
                        if i == 8:
                            act.wait_ge(weights_free, n * TILES + 3)
                        act.wait_ge(score_full, n * NS + i + 1)
                        at = kb % 2 * PER
                        act.activation(weights[:, at + heads[0]:at + heads[-1] + 1, 0:cols],
                                       score_ps[i % 2][:, :].rearrange("p (h c) -> p h c", c=cols), ACT.Exp).then_inc(score_free, 1)
                        if g == 0 and i == 3:
                            move_heads(b)
                        if i == (1 if g else 3):
                            round_projection(misc)
                        if i == 5:
                            set_apart((g + 2) % GROUPS, misc + 2)
                        if i == 6:
                            round_projection(misc + 1)
                    act.wait_ge(weights_free, (n + 1) * TILES + 2)
                    act.copy(sums_t[:, :], sums_ps[:, :]).then_inc(sums_moved, 1)
            move_heads(B)

        @block.vector
        def _(dve):
            V = nc.vector
            dve.sem_inc(misc_free, 1)
            dve.sem_inc(max_free, 2)
            dve.sem_inc(result_out, 32)
            dve.wait_ge(weights_in, 7 * 16)
            V.scalar_tensor_tensor(aux_const[:, 0, :], aux_raw[:, 0, :], DH ** -0.5, aux_const[:, 0, :], ALU.mult, ALU.add)
            V.tensor_tensor(aux_const[:, 1, :], aux_raw[:, 1, :], aux_const[:, 1, :], ALU.add).then_inc(aux_summed, 1)
            dve.wait_ge(weights_rounded, 1)
            V.tensor_tensor(wk[1][:, :], wk_raw, wk[0][:, :].bitcast(F32), ALU.subtract)
            dve.wait_ge(aux_summed, 1)
            dve.wait_ge(aux_rounded, 1)
            V.scalar_tensor_tensor(aux[:, :, :], aux[:, :, :].bitcast(F32), const[0:3, C_NEG_AUX:C_NEG_AUX + 1],
                                   aux_const, ALU.mult, ALU.add).then_inc(weights_split, 1)
            for n, raw, (hi, lo) in ((2, wq_raw, wq), (3, wv_raw, wv)):
                dve.wait_ge(weights_rounded, n)
                V.tensor_tensor(lo[:, :], raw, hi[:, :].bitcast(F32), ALU.subtract).then_inc(weights_split, 1)

            def split_projection(out, neg, n):
                dve.wait_ge(qk_rounded, n + 1)
                V.scalar_tensor_tensor(out[:, :], rounded[:, :].bitcast(F32), const[:, neg:neg + 1],
                                       misc_ps[:, :], ALU.mult, ALU.add).then_inc(misc_free, 1)

            def maximum(g, n, i):
                tiles, heads = MAXIMA[i]
                dve.wait_ge(max_full, n * NM + i + 1)
                ps = max_ps[(g + i) % 2]
                if tiles == (1,):
                    V.tensor_reduce(neg_max[g % 2][:, 1, :], ps[:, :, :].rearrange("p a (h k) -> p (a h) k", k=2 * P), AX.X, ALU.max, negate=True).then_inc(max_free, 1)
                    return
                at = 0
                for qb in tiles:
                    last = V.tensor_reduce(neg_max[g % 2][:, qb, heads[0]:heads[-1] + 1], ps[:, :, at:at + (qb + 1) * P], AX.X, ALU.max, negate=True)
                    at += (qb + 1) * P
                last.then_inc(max_free, 1)

            def split_maxima(g, n):
                cols = max_cols[:, :, :].rearrange("p t (h r) -> p t h r", r=32)
                dve.wait_ge(max_free, (n + 1) * NM + 2)
                V.tensor_copy(cols[:, :, :, 28], neg_max[g % 2][:, :, :]).then_inc(max_high, 1)
                dve.wait_ge(max_high, n + 1)
                V.tensor_tensor(cols[:, :, :, 29], neg_max[g % 2][:, :, :], cols[:, :, :, 28].bitcast(F32), ALU.subtract).then_inc(max_split, 1)

            def move_values(misc):
                dve.wait_ge(misc_full, misc + 1)
                bias = bv[:, :].rearrange("p (h d) -> p h d", d=DH).unsqueeze(1).to_broadcast([P, TILES, HEADS, DH])
                V.tensor_tensor(values[:, :, :, 0:DH], misc_ps[:, :].rearrange("p (t h d) -> p t h d", t=TILES, d=DH), bias, ALU.add).then_inc(misc_free, 1)

            def add_maxima(g, misc):
                dve.wait_ge(misc_full, misc + 1)
                V.tensor_tensor(qm_rows[g % 2][:, :], misc_ps[:, :], q_rows[g % 2][:, :].bitcast(F32), ALU.add).then_inc(misc_free, 1)

            def set_apart(g, split):
                dve.wait_ge(misc_free, split)
                for j in range(PER - 1):
                    rows = slice(32 * j, 32 * j + 32)
                    last = V.tensor_copy(k_apart[g][rows, j, :], k_rows[g % 2][rows, :].bitcast(F32))
                last.then_inc(first_apart, 1)

            def divide(g, n):
                dve.wait_ge(sums_turned, n + 1)
                turned = sums_ps[:, :].rearrange("p (t h r) -> p t h r", t=TILES, r=32)
                V.reciprocal(divisor[:, :, :], turned[:, :, :, DH]).then_inc(has_divisor, 1)
                dve.wait_ge(has_divisor, n + 1)
                out = heads_out[:, :, g * 32:(g + 1) * 32].rearrange("p t (h d) -> p t h d", d=DH)
                V.tensor_tensor(out, turned[:, :, :, 0:DH], divisor[:, :, :].unsqueeze(3).to_broadcast([P, TILES, PER, DH]), ALU.mult).then_inc(divided, 1)

            def add_up(b):
                dve.wait_ge(projected, b + 1)
                dve.wait_ge(result_out, (b + 1) * 16)
                V.tensor_tensor(result[:, :, :], sums_ps[:, :].rearrange("p (t d) -> p t d", t=TILES),
                                rows_of(x_rows, b - 1), ALU.add).then_inc(result_full, 1)

            dve.wait_ge(zeroed, 8)
            for g in range(2):
                split_projection(k_rows[g], C_NEG_K, 2 * g)
                set_apart(g, 2 * g + 2)
                if g:
                    maximum(0, 0, 2)
                    maximum(0, 0, 3)
                split_projection(q_rows[g], C_NEG_Q, 2 * g + 1)
                maximum(0, 0, 4 * g)
                if g == 0:
                    maximum(0, 0, 1)
            split_maxima(0, 0)
            add_maxima(0, 4)
            maximum(1, 1, 0)
            maximum(1, 1, 1)
            dve.wait_ge(ones_set, 2)
            move_values(5)
            with dve.Fori(0, B) as b:
                misc0 = b * MISC_SEQ + MISC_EARLY
                for g in range(GROUPS):
                    n = b * GROUPS + g
                    misc = misc0 + g * MISC_GROUP
                    new = g % 2
                    divide((g + 3) % GROUPS, n)
                    maximum(g + 1, n + 1, 2)
                    if g == 0:
                        maximum(g + 1, n + 1, 3)
                    dve.wait_ge(first_apart, n + 1)
                    dve.wait_ge(last_apart, n + 1)
                    split_projection(k_rows[new], C_NEG_K, n * 2 + 4)
                    if g == 0:
                        add_up(b)
                    else:
                        maximum(g + 1, n + 1, 3)
                    set_apart((g + 2) % GROUPS, misc + 2)
                    maximum(g + 1, n + 1, 4)
                    split_projection(q_rows[new], C_NEG_Q, n * 2 + 5)
                    split_maxima(g + 1, n + 1)
                    add_maxima((g + 1) % GROUPS, misc + 2)
                    maximum(g + 2, n + 2, 0)
                    maximum(g + 2, n + 2, 1)
                move_values(misc0 + GROUPS * MISC_GROUP)
            divide(GROUPS - 1, B * GROUPS)
            add_up(B)

        @block.tensor
        def _(pe):
            pe.sem_inc(weights_free, 2)

            def turn_sums(n):
                pe.wait_ge(sums_moved, n + 1)
                for i in range(TILES):
                    last = pe.transpose(sums_ps[:, i * P:(i + 1) * P], sums_t[:, i * P:(i + 1) * P], ident)
                last.then_inc(sums_turned, 1)

            def scores(g, n, i):
                tiles, heads = SCORES[i]
                pe.wait_ge(score_free, n * NS + i + 1)
                out = score_ps[i % 2]
                at = 0
                for kb in tiles:
                    cols = S - kb * P
                    for head in heads:
                        pe.matmul(out[:, at:at + cols], k_apart[g][:, head, kb * P:(kb + 1) * P], qm_rows[g % 2][:, kb * P:], start=at == 0, stop=False)
                        at += cols
                if tiles == (0,):
                    diagonals, count = out[:, 0:P], 1
                elif tiles == (3, 1):
                    diagonals, count = out[:, 0:2 * P], 2
                else:
                    diagonals, count = out[:, :].rearrange("p (h c) -> p h c", c=2 * P)[:, :, 0:P], 2
                masked(diagonals, 1, count).then_inc(score_full, 1)

            def turn_heads(b):
                pe.wait_ge(divided, b * GROUPS + 1)
                for i in range(TILES):
                    last = pe.transpose(sums_ps[:, i * P:(i + 1) * P], heads_out[:, i, :], ident)
                last.then_inc(heads_turned, 1)

            def project_output(b):
                pe.wait_ge(heads_moved, b + 1)
                for i in range(TILES):
                    at = slice(i * P, (i + 1) * P)
                    last = pe.matmul(sums_ps[:, at], heads_out_t[:, at], wo[:, :], start=True, stop=True)
                last.then_inc(projected, 1)

            def three_passes(out, lhs, rhs, stop=False):
                pe.matmul(out, lhs[0], rhs[0], start=True, stop=False)
                pe.matmul(out, lhs[0], rhs[1], start=False, stop=False)
                return pe.matmul(out, lhs[1], rhs[0], start=False, stop=stop)

            def project(w, which, g, misc):
                at = slice(g * P, (g + 1) * P)
                pe.wait_ge(misc_free, misc + 1)
                three_passes(misc_ps[:, :], [w[0][:, at], w[1][:, at]], [x_seq[0][:, :], x_seq[1][:, :]])
                pe.matmul(misc_ps[:, :], aux[:, which, at], aux_rows[:, :], start=False, stop=True).then_inc(misc_full, 1)

            def masked(diagonals, which, count):
                if len(diagonals.shape) == 2:
                    diagonals = diagonals.rearrange("p (h c) -> p h c", c=P)
                return pe.matmul(diagonals, ident_r[:, :], masks[:, which, :].unsqueeze(1).to_broadcast([P, count, P]), start=False, stop=True)

            def maxima(g, n, i):
                tiles, heads = MAXIMA[i]
                pe.wait_ge(max_free, n * NM + i + 1)
                each = len(heads) // 2
                for a in range(2):
                    out = max_ps[(g + i) % 2][:, a, :]
                    at = 0
                    for qb in tiles:
                        for head in heads[a * each:(a + 1) * each]:
                            pe.matmul(out[:, at:at + (qb + 1) * P], q_rows[g % 2][:, qb * P:(qb + 1) * P], k_apart[g][:, head, 0:(qb + 1) * P],
                                      start=at == 0, stop=False)
                            at += (qb + 1) * P
                    if tiles == (3,):
                        diagonals, count = out[:, 3 * P:S], 1
                    elif tiles == (2, 0):
                        diagonals, count = out[:, 2 * P:S], 2
                    else:
                        diagonals, count = out.rearrange("p (h k) -> p h k", k=2 * P)[:, :, P:2 * P], 2
                    last = masked(diagonals, 0, count)
                last.then_inc(max_full, 1)

            def turn_maxima(n, misc):
                pe.wait_ge(max_split, n + 1)
                pe.wait_ge(misc_free, misc + 1)
                for i in range(TILES):
                    last = pe.matmul(misc_ps[:, i * P:(i + 1) * P], max_cols[:, i, :], ident_r[:, :], start=True, stop=True)
                last.then_inc(misc_full, 1)

            def project_values(misc):
                pe.wait_ge(misc_free, misc + 1)
                for i in range(TILES):
                    at = slice(i * P, (i + 1) * P)
                    out = misc_ps[:, at]
                    last = three_passes(out, [x_seq[0][:, at], x_seq[1][:, at]], [wv[0][:, :], wv[1][:, :]], stop=True)
                last.then_inc(misc_full, 1)

            def multiply(g, n, kb):
                pe.wait_ge(score_free, n * NS + scored[kb] + 2)
                begin = P if kb == 1 else 0
                for j in range(PER):
                    last = pe.matmul(sums_ps[32 * j:32 * j + 32, kb * P:], values[:, kb, g * PER + j, :],
                                     weights[:, kb % 2 * PER + j, begin:begin + S - kb * P], start=kb == 0, stop=kb == 2)
                last.then_inc(weights_free, 1)

            for _ in range(WARM):
                pe.matmul(misc_ps[:, :], xt_hi[:, 0:P], xt_hi[:, 0:S], start=True, stop=True)
            pe.wait_ge(weights_split, 1)
            pe.wait_ge(ones_set, 2)
            pe.wait_ge(seq_in, 32)
            project(wk, 1, 0, 0)
            pe.wait_ge(weights_split, 2)
            project(wq, 0, 0, 1)
            pe.wait_ge(misc_free, 3)
            pe.wait_ge(first_apart, 1)
            pe.wait_ge(last_apart, 1)
            project(wk, 1, 1, 2)
            maxima(0, 0, 0)
            maxima(0, 0, 1)
            maxima(0, 0, 2)
            maxima(0, 0, 3)
            project(wq, 0, 1, 3)
            maxima(0, 0, 4)
            turn_maxima(0, 4)
            pe.wait_ge(misc_free, 5)
            pe.wait_ge(first_apart, 2)
            pe.wait_ge(last_apart, 2)
            for i in range(2):
                maxima(1, 1, i)
            pe.wait_ge(weights_split, 3)
            project_values(5)
            with pe.Fori(0, B) as b:
                misc0 = b * MISC_SEQ + MISC_EARLY
                for g in range(GROUPS):
                    n = b * GROUPS + g
                    misc = misc0 + g * MISC_GROUP
                    pe.wait_ge(misc_free, misc if g == 0 else misc + 1)
                    new = (g + 2) % GROUPS

                    def project_keys():
                        if g == 2:
                            pe.wait_ge(seq_in, (b + 2) * 32)
                        project(wk, 1, new, misc)

                    scores(g, n, 0)
                    scores(g, n, 1)
                    if g:
                        project_keys()
                    turn_sums(n)
                    maxima((g + 1) % GROUPS, n + 1, 2)
                    scores(g, n, 2)
                    scores(g, n, 3)
                    maxima((g + 1) % GROUPS, n + 1, 3)
                    if g == 0:
                        turn_heads(b)
                        project_keys()
                    scores(g, n, 4)
                    scores(g, n, 5)
                    if g == 0:
                        project_output(b)
                    else:
                        pe.wait_ge(divided, n + 1)
                        multiply(g, n, 0)
                    scores(g, n, 6)
                    scores(g, n, 7)
                    project(wq, 0, new, misc + 1)
                    maxima((g + 1) % GROUPS, n + 1, 4)
                    if g == 0:
                        pe.wait_ge(result_full, b + 1)
                        pe.wait_ge(misc_free, misc + 1)
                        multiply(g, n, 0)
                    scores(g, n, 8)
                    multiply(g, n, 1)
                    scores(g, n, 9)
                    multiply(g, n, 3)
                    pe.wait_ge(misc_free, misc + 3)
                    pe.wait_ge(first_apart, n + 3)
                    pe.wait_ge(last_apart, n + 3)
                    maxima(new, n + 2, 0)
                    turn_maxima(n + 1, misc + 2)
                    multiply(g, n, 2)
                    maxima(new, n + 2, 1)
                project_values(misc0 + GROUPS * MISC_GROUP)
            turn_sums(B * GROUPS)
            turn_heads(B)
            project_output(B)


def constants():
    c = np.zeros((P, C_END), np.float32)
    p = np.arange(P)
    c[:, C_IDENT:C_IDENT + P] = np.eye(P)
    c[E:2 * E, C_NEG_W] = -1
    row = p % 32
    c[(row >= 20) & (row < 28), C_NEG_Q] = -1
    c[(row >= 12) & (row < 20), C_NEG_K] = -1
    c[1, C_NEG_AUX] = -1
    c[:, C_RANK:C_RANK + TILES * N_GROUP] = 2 - np.tile(np.arange(N_GROUP), TILES)
    c[:, C_POW:C_POW + TILES] = -0.5
    c[:, C_MASK_Q:C_MASK_Q + P] = np.where(p[None, :] > p[:, None], -1e30, 0)
    c[:, C_MASK_K:C_MASK_K + P] = np.where(p[:, None] > p[None, :], -1e30, 0)
    c[0:2, C_AUX:] = 1
    c[2, C_AUX:] = np.arange(S)
    return c


def attention_constants():
    start = 2 ** (-2 ** (-(np.log2(HEADS) - 3)))
    slopes = np.array([start * start ** i for i in range(HEADS)], np.float32)
    bits = slopes.view(np.uint32)
    high = ((bits + 0x7ff + ((bits >> 12) & 1)) & np.uint32(0xfffff000)).view(np.float32)
    low = slopes - high
    c = np.zeros((3, 2, HEADS, 32), np.float32)
    q, k = c[:, 0], c[:, 1]
    q[0:2, :, 0], q[0:2, :, 2] = high, low
    k[0:2, :, 1], k[0:2, :, 3] = -high, -low
    q[2, :, [1, 3]] = 1
    k[2, :, [0, 2]] = 1
    k[0:2, :, 28:30] = 1
    return c.reshape(3, 2, HEADS * 32)


def program(nc, dram):
    with ExitStack() as ctx:
        def sb(name, shape, dt=F32):
            return ctx.enter_context(nc.sbuf_tensor(name, shape, dt))

        t = {
            "x_rows": sb("x_rows", [P, (B + 2) * TILES, D]),
            "xt_hi": sb("xt_hi", [P, (B + 1) * S], F32R),
            "xt_lo": sb("xt_lo", [P, (B + 1) * S], F32R),
            "const": sb("const", [P, C_END]),
        }
        expert_phase(nc, t, dram)
        attention_phase(nc, t, dram)


def layout(a):
    f = {k: np.asarray(v) for k, v in a.items()}
    pair = lambda w, shared: np.concatenate([shared.T, w.transpose(2, 0, 1).reshape(D, E * I)], axis=1)
    down = f["L0_ffn_expert_down"].transpose(0, 2, 1).reshape(PAIRS, P, D).transpose(1, 0, 2)
    pick = np.zeros((2 * E, PAIRS, P), np.float32)
    for e in range(E):
        pick[[e, E + e], e // 2, (e % 2) * I:(e % 2 + 1) * I] = 1

    def padded(w, starts):
        out = np.zeros((w.shape[0], HEADS, 32), np.float32)
        for at in starts:
            out[:, :, at:at + DH] = w.reshape(-1, HEADS, DH)
        return out.reshape(-1, HEADS * 32)

    aux_bias = np.zeros((3, 2, HEADS * 32), np.float32)
    aux_bias[0:2, 0] = padded(f["L0_attn_bq"].reshape(1, D), (4, 12, 20))
    aux_bias[0:2, 1] = padded(f["L0_attn_bk"].reshape(1, D), (4, 12, 20))
    return {
        "x": f["L0_attn_x"].reshape(B * S, D),
        "const": constants(),
        "gate_w": f["L0_ffn_gate_w"].T,
        "gate_b": np.broadcast_to(f["L0_ffn_gate_bias"], (P, TILES, E)),
        "bo": f["L0_attn_bo"].reshape(D, 1),
        "pick": pick.reshape(2 * E, PAIRS * P),
        "wq": padded(f["L0_attn_Wq"].T, (4, 12, 20)),
        "wk": padded(f["L0_attn_Wk"].T, (4, 12, 20)),
        "wv": f["L0_attn_Wv"].T,
        "wo": f["L0_attn_Wo"].T,
        "bv": np.broadcast_to(f["L0_attn_bv"], (P, D)),
        "aux_bias": aux_bias,
        "aux_const": attention_constants(),
        "wg": pair(f["L0_ffn_expert_gate"], f["L0_ffn_shared_gate"]),
        "wu": pair(f["L0_ffn_expert_up"], f["L0_ffn_shared_up"]),
        "wd": np.concatenate([f["L0_ffn_shared_down"].T[:, None, :], down], axis=1).reshape(P, UNITS * D),
    }


def build(nc, arrays):
    dram = {n: nc.dram_tensor("in_" + n, a.shape, mybir.dt.from_np(a.dtype), kind="ExternalInput").ap() for n, a in arrays.items()}
    dram["x"] = dram["x"].rearrange("(n p) d -> p n d", p=P)
    dram["out"] = nc.dram_tensor("out", (B, S, D), F32, kind="ExternalOutput").ap().rearrange("b (n p) d -> p (b n) d", p=P)
    program(nc, dram)


def kernel(**inputs):
    import concourse.bacc as bacc
    from concourse.bass_utils import run_bass_kernel_spmd

    nc = bacc.Bacc("TRN2", target_bir_lowering=False, num_devices=1)
    arrays = {n: np.ascontiguousarray(a) for n, a in layout(inputs).items()}
    build(nc, arrays)
    r = run_bass_kernel_spmd(nc, [{"in_" + n: a for n, a in arrays.items()}], core_ids=[0])
    return r.results[0]["out"]
```
